# Optimizing a Trainium2 kernel written in Bass

```python
import numpy as np
import jax
import jax.numpy as jnp

def _softmax(x, axis=-1):
    return jax.nn.softmax(x, axis=axis)

def _gelu(x):
    return jax.nn.gelu(x, approximate=True)

def _silu(x):
    return jax.nn.silu(x)

def _sigmoid(x):
    return jax.nn.sigmoid(x)

def _layernorm(x, axis=-1, eps=1e-05):
    m = jnp.mean(x, axis=axis, keepdims=True)
    v = jnp.var(x, axis=axis, keepdims=True)
    return (x - m) / jnp.sqrt(v + eps)

def _scatter_add(tgt, idx, src, axis=0):
    return tgt.at[idx].add(src)

def _segment_sum(src, seg, n):
    return jax.ops.segment_sum(src, seg, n)
kernel_name = 'mk_lm_tower_d1_tok_ids2048_r4_bf9a18'

def setup_inputs(seed: int=0):
    np.random.seed(seed)
    _w = jnp.asarray

    def _rec_inputs():
        import jax
        import jax.numpy as jnp
        _rk = jax.random.key(seed)
        x = jax.random.randint(jax.random.fold_in(_rk, 1), (16, 512), 0, 8000, jnp.int32)
        return x
    x = _rec_inputs()

    def _L0_tok_setup():
        import jax, jax.numpy as jnp
        import numpy as np
        VOCAB = 8000
        DIM = 64
        key = jax.random.key(seed)
        k1, k2 = jax.random.split(key)
        sequence = jax.random.randint(k1, (16, 512), 0, VOCAB, dtype=jnp.int64 if jax.config.jax_enable_x64 else jnp.int32)
        weight = jax.random.normal(k2, (VOCAB, DIM), dtype=jnp.float32)
        return {'sequence': sequence, 'weight': weight}
    _L0_tok_all = _L0_tok_setup()
    _L0_tok_in = {k: v for k, v in _L0_tok_all.items() if k in ('weight',)}
    del _L0_tok_all

    def _L0_attn_setup():
        import jax, jax.numpy as jnp
        import numpy as np
        B, T, D, S = (8, 1024, 512, 128)

        def _layernorm(x, gamma, beta, eps=1e-05):
            mu = jnp.mean(x, axis=-1, keepdims=True)
            var = jnp.var(x, axis=-1, keepdims=True)
            return (x - mu) * jax.lax.rsqrt(var + eps) * gamma + beta
        key = jax.random.key(seed)
        ks = jax.random.split(key, 9)
        sd = 0.02
        return {'x': jax.random.normal(ks[0], (B, T, D), dtype=jnp.float32), 'gamma': jnp.ones((D,), dtype=jnp.float32), 'beta': jnp.zeros((D,), dtype=jnp.float32), 'W_in': jax.random.normal(ks[1], (D, 3 * S), dtype=jnp.float32) * sd, 'b_in': jnp.zeros((3 * S,), dtype=jnp.float32), 'W_out': jax.random.normal(ks[2], (S, D), dtype=jnp.float32) * sd, 'b_out': jnp.zeros((D,), dtype=jnp.float32), 'W_skip': jax.random.normal(ks[3], (D, D), dtype=jnp.float32) * sd, 'b_skip': jnp.zeros((D,), dtype=jnp.float32)}
    _L0_attn_all = _L0_attn_setup()
    _L0_attn_in = {k: v for k, v in _L0_attn_all.items() if k in ('gamma', 'beta', 'W_in', 'b_in', 'W_out', 'b_out', 'W_skip', 'b_skip')}
    del _L0_attn_all

    def _L0_ffn_setup():
        import jax, jax.numpy as jnp
        import numpy as np
        TURBO_BLOCK_SIZE = 64
        TURBO_MSE_BITS = 5
        QMAX = 2 ** (TURBO_MSE_BITS - 1) - 1
        SHRINKS = np.linspace(0.4, 1.0, 16)

        def mse_quant_dequant(w):
            O, I = w.shape
            wb = w.reshape(O, I // TURBO_BLOCK_SIZE, TURBO_BLOCK_SIZE)
            amax = jnp.max(jnp.abs(wb), axis=-1, keepdims=True)
            base = jnp.maximum(amax, 1e-08) / QMAX
            best_err = jnp.full(amax.shape, jnp.inf, dtype=w.dtype)
            best_scale = base
            for s in SHRINKS:
                scale = base * jnp.asarray(s, dtype=w.dtype)
                deq = jnp.clip(jnp.round(wb / scale), -QMAX, QMAX) * scale
                err = jnp.sum((deq - wb) ** 2, axis=-1, keepdims=True)
                upd = err < best_err
                best_err = jnp.where(upd, err, best_err)
                best_scale = jnp.where(upd, scale, best_scale)
            deq = jnp.clip(jnp.round(wb / best_scale), -QMAX, QMAX) * best_scale
            return deq.reshape(O, I)

        def turbo_linear(x, w):
            wq = w + jax.lax.stop_gradient(mse_quant_dequant(w) - w)
            return x @ wq.T
        key = jax.random.key(seed)
        k1, k2, k3 = jax.random.split(key, 3)
        dim, mlp_mult = (512, 4)
        hidden = mlp_mult * dim
        x = jax.random.normal(k1, (4, 512, dim), dtype=jnp.float32)
        w_fc = jax.random.normal(k2, (hidden, dim), dtype=jnp.float32) * 0.02
        w_proj = jax.random.normal(k3, (dim, hidden), dtype=jnp.float32) * 0.02
        return {'x': x, 'w_fc': w_fc, 'w_proj': w_proj}
    _L0_ffn_all = _L0_ffn_setup()
    _L0_ffn_in = {k: v for k, v in _L0_ffn_all.items() if k in ('w_fc', 'w_proj')}
    del _L0_ffn_all
    return {'x': x, 'L0_tok_weight': _L0_tok_in['weight'], 'L0_attn_gamma': _L0_attn_in['gamma'], 'L0_attn_beta': _L0_attn_in['beta'], 'L0_attn_W_in': _L0_attn_in['W_in'], 'L0_attn_b_in': _L0_attn_in['b_in'], 'L0_attn_W_out': _L0_attn_in['W_out'], 'L0_attn_b_out': _L0_attn_in['b_out'], 'L0_attn_W_skip': _L0_attn_in['W_skip'], 'L0_attn_b_skip': _L0_attn_in['b_skip'], 'L0_ffn_w_fc': _L0_ffn_in['w_fc'], 'L0_ffn_w_proj': _L0_ffn_in['w_proj']}

def reference(x, L0_tok_weight, L0_attn_gamma, L0_attn_beta, L0_attn_W_in, L0_attn_b_in, L0_attn_W_out, L0_attn_b_out, L0_attn_W_skip, L0_attn_b_skip, L0_ffn_w_fc, L0_ffn_w_proj):
    import jax
    import jax.numpy as jnp

    def _L0_tok_ref(sequence, weight):
        import jax, jax.numpy as jnp
        import numpy as np
        VOCAB = 8000
        DIM = 64
        embs = weight[sequence]
        bias = jnp.einsum('bsd,btd->bst', embs, embs) / jnp.sqrt(jnp.asarray(DIM, embs.dtype))
        return bias

    def _L0_attn_ref(x, gamma, beta, W_in, b_in, W_out, b_out, W_skip, b_skip):
        import jax, jax.numpy as jnp
        import numpy as np
        B, T, D, S = (8, 1024, 512, 128)

        def _layernorm(x, gamma, beta, eps=1e-05):
            mu = jnp.mean(x, axis=-1, keepdims=True)
            var = jnp.var(x, axis=-1, keepdims=True)
            return (x - mu) * jax.lax.rsqrt(var + eps) * gamma + beta
        u = _layernorm(x, gamma, beta)
        gates = jnp.einsum('btd,de->bte', u, W_in) + b_in
        S_ = W_out.shape[0]
        delta, b_proj, c_proj = (gates[..., :S_], gates[..., S_:2 * S_], gates[..., 2 * S_:])
        alpha = jax.nn.sigmoid(delta)
        tc = jnp.tanh(c_proj)

        def step(h, inp):
            a_t, b_t, tc_t = inp
            h = (1.0 - a_t) * h + a_t * b_t
            return (h, h * tc_t)
        h0 = jnp.zeros((x.shape[0], S_), dtype=x.dtype)
        _, y = jax.lax.scan(step, h0, (alpha.transpose(1, 0, 2), b_proj.transpose(1, 0, 2), tc.transpose(1, 0, 2)))
        y = y.transpose(1, 0, 2)
        out = jnp.einsum('bts,sd->btd', y, W_out) + b_out
        out = out + jnp.einsum('btd,de->bte', x, W_skip) + b_skip
        return out

    def _L0_ffn_ref(x, w_fc, w_proj):
        import jax, jax.numpy as jnp
        import numpy as np
        TURBO_BLOCK_SIZE = 64
        TURBO_MSE_BITS = 5
        QMAX = 2 ** (TURBO_MSE_BITS - 1) - 1
        SHRINKS = np.linspace(0.4, 1.0, 16)

        def mse_quant_dequant(w):
            O, I = w.shape
            wb = w.reshape(O, I // TURBO_BLOCK_SIZE, TURBO_BLOCK_SIZE)
            amax = jnp.max(jnp.abs(wb), axis=-1, keepdims=True)
            base = jnp.maximum(amax, 1e-08) / QMAX
            best_err = jnp.full(amax.shape, jnp.inf, dtype=w.dtype)
            best_scale = base
            for s in SHRINKS:
                scale = base * jnp.asarray(s, dtype=w.dtype)
                deq = jnp.clip(jnp.round(wb / scale), -QMAX, QMAX) * scale
                err = jnp.sum((deq - wb) ** 2, axis=-1, keepdims=True)
                upd = err < best_err
                best_err = jnp.where(upd, err, best_err)
                best_scale = jnp.where(upd, scale, best_scale)
            deq = jnp.clip(jnp.round(wb / best_scale), -QMAX, QMAX) * best_scale
            return deq.reshape(O, I)

        def turbo_linear(x, w):
            wq = w + jax.lax.stop_gradient(mse_quant_dequant(w) - w)
            return x @ wq.T
        h = jnp.maximum(turbo_linear(x, w_fc), 0.0)
        return turbo_linear(h * h, w_proj)
    h = _L0_tok_ref(x, L0_tok_weight)
    h = h + _L0_attn_ref(_layernorm(h, axis=-1), L0_attn_gamma, L0_attn_beta, L0_attn_W_in, L0_attn_b_in, L0_attn_W_out, L0_attn_b_out, L0_attn_W_skip, L0_attn_b_skip)
    h = h + _L0_ffn_ref(_layernorm(h, axis=-1), L0_ffn_w_fc, L0_ffn_w_proj)
    return h

_drawn_inputs = setup_inputs


def setup_inputs(seed=0):
    import zlib

    import numpy as np

    out = dict(_drawn_inputs(seed))
    spreads = {'L0_attn_gamma': (1.0, 0.6),
     'L0_attn_beta': (0.0, 0.8),
     'L0_attn_b_in': (0.0, 0.8),
     'L0_attn_b_out': (0.0, 0.1),
     'L0_attn_b_skip': (0.0, 0.1)}
    factors = {}
    for name, (base, spread) in spreads.items():
        noise = np.random.default_rng([zlib.crc32(name.encode()), seed]).standard_normal(out[name].shape)
        drawn = base * np.exp(spread * noise) if base else spread * noise
        out[name] = jnp.asarray(drawn.astype(out[name].dtype))
    for name, factor in factors.items():
        out[name] = (out[name] * factor).astype(out[name].dtype)
    return out
```

```python
from contextlib import ExitStack

import numpy as np

import concourse.bass as bass
from concourse import mybir

ALU = mybir.AluOpType
ACT = mybir.ActivationFunctionType
AX = mybir.AxisListType.X
F32 = mybir.dt.float32
BF16 = mybir.dt.bfloat16
U32 = mybir.dt.uint32

P = 128
SEQS, TOK, EMB = 16, 512, 64
D = TOK
S = 128
KT = TOK // P
KD = D // P
GATES = 3 * S
HID = 4 * D
PAIRS = SEQS // 2

PHASES = 4
HPP = HID // PHASES
HC = HPP // P
UNITS = PHASES * PAIRS
HALF = 256
UW = 2 * HALF
QB = 64
NB = UW // QB
UT = UW // P

QMAX = 15.0
MAGIC = 1.5 * 2.0 ** 23
SHRINKS = [float(np.float32(s)) for s in np.linspace(0.4, 1.0, 16)]
NS = len(SHRINKS)
EPS = 1e-5
RING = 3


def build(nc, ids, table, gamma, beta, w_in, b_in, w_out, b_out, w_skip, b_skip, w_fc, w_proj, out):
    ctx = ExitStack()
    with ctx:
        def sb(name, shape, dt=F32):
            return ctx.enter_context(nc.sbuf_tensor(name, shape, dt))

        def sem(name):
            return ctx.enter_context(nc.semaphore(name))

        xt_dram = nc.dram_tensor("xt_dram", [SEQS, P, 2 * KD * TOK], BF16).ap()
        acc_dram = nc.dram_tensor("acc_dram", [SEQS, P, KT * D], F32).ap()

        ident = sb("ident", [P, P])
        ones_mean = sb("ones_mean", [P, P])
        magic = sb("magic", [P, 1])
        neg_half = sb("neg_half", [P, 2 * KT])
        eps = sb("eps", [P, 2 * KT])
        neg_one = sb("neg_one", [P, KT])
        idx_seen = sb("idx_seen", [P, 1])
        shrink_val = sb("shrink_val", [P, NS])
        shrink_rank = sb("shrink_rank", [P, NS])
        idx = sb("idx", [P, SEQS * KT], U32)
        wc = sb("wc", [P, KT, GATES + D])
        w_out_sb = sb("w_out_sb", [P, D])
        gamma_sb = sb("gamma_sb", [P, KD])
        beta_sb = sb("beta_sb", [P, KD])
        b_in_sb = sb("b_in_sb", [P, 3])
        c_in = sb("c_in", [P, 3])
        bias_bc = sb("bias_bc", [P, D])

        idx_now = sb("idx_now", [P, 2 * KT], U32)
        emb_next = sb("emb_next", [P, 2 * KT, EMB])
        emb2 = sb("emb2", [P, 2 * KT, 2, EMB])
        emb_c = sb("emb_c", [P, 2 * KT, EMB])
        lhs = sb("lhs", [P, 2, TOK])
        rhs = sb("rhs", [P, 2, D])
        gate_w = sb("gate_w", [P, 2, GATES])
        gate_x = sb("gate_x", [P, 2, TOK])
        cov = sb("cov", [EMB, 2, EMB])
        quad = sb("quad", [P, 2 * KT, EMB])
        scaled = sb("scaled", [P, 2 * KT, 2, EMB])
        var1 = sb("var1", [P, 2 * KT])
        stat = sb("stat", [P, 8, 2 * KT])
        mix = sb("mix", [P, 2, 4, TOK])
        gate_y = sb("gate_y", [P, 2, TOK])
        bn6 = sb("bn6", [P, 2 * KT, 6])
        mean_var = sb("mean_var", [P, 2 * KT, 2])
        stat3 = sb("stat3", [P, 2, 4, KT])
        res = sb("res", [P, 2, KT, D])
        xt = sb("xt", [P, 2, 2, KD, TOK], BF16)

        w_hi = sb("w_hi", [P, UNITS, UW], BF16)
        w_lo = sb("w_lo", [P, UNITS, UW], BF16)
        w_raw = sb("w_raw", [P, UW])
        w_abs = sb("w_abs", [P, UW])
        w_norm = sb("w_norm", [P, UW])
        q_mag = sb("q_mag", [P, RING, UW])
        q_int = sb("q_int", [P, RING, UW], BF16)
        q_dif = sb("q_dif", [P, RING, UW])
        q_sq = sb("q_sq", [P, RING, UW])
        err = sb("err", [P, NS, NB])
        pick = sb("pick", [P, 2, NS, NB])
        qs = sb("qs", [P, 8, NB])
        w_q = sb("w_q", [P, UW])

        g_hi = sb("g_hi", [P, 2, TOK], BF16)
        g_lo = sb("g_lo", [P, 2, TOK], BF16)
        relu_z = mix[:, 0, 0:2, :]
        act_g = mix[:, 0, 2:4, :]

        bank = [ctx.enter_context(nc.psum_tensor(f"bank{i}", [P, 512], F32)) for i in range(8)]
        Q_BANK = 7
        PROJ_BANK = ((4, 5), (0, 6))
        GATE_BANK = ((4, 5, 6), (0, 1, 3))
        H2_BANK = (4, 5, 6, 2, 0, 1, 3, 4)
        XT_BANK = (5, 6, 2, 1, 0, 3, 4, 5)

        consts_in = sem("consts_in")
        idx_in = sem("idx_in")
        pool_const = sem("pool_const")
        zero_gate = sem("zero_gate")
        bias_done = sem("bias_done")
        cin_ps = sem("cin_ps")
        wg_ready = sem("wg_ready")
        wmean_ps = sem("wmean_ps")
        wc_ready = sem("wc_ready")
        cin_ready = sem("cin_ready")
        emb_in = sem("emb_in")
        idx_ready = sem("idx_ready")
        emb2_ready = sem("emb2_ready")
        mean_ps = sem("mean_ps")
        et_ps = sem("et_ps")
        et_sb = sem("et_sb")
        emb_c_ready = sem("emb_c_ready")
        cov_ps = sem("cov_ps")
        cov_sb = sem("cov_sb")
        quad_ps = sem("quad_ps")
        proj_ps = sem("proj_ps")
        gate_w_ready = sem("gate_w_ready")
        skip_ready = sem("skip_ready")
        var1_ready = sem("var1_ready")
        r12_ready = sem("r12_ready")
        scaled_ready = sem("scaled_ready")
        scaled_ps = sem("scaled_ps")
        gate_x_ready = sem("gate_x_ready")
        gates_ps = sem("gates_ps")
        alpha_ready = sem("alpha_ready")
        tanh_ready = sem("tanh_ready")
        y_ready = sem("y_ready")
        h2_ps = sem("h2_ps")
        h2_sb = sem("h2_sb")
        mv_ready = sem("mv_ready")
        r3_ready = sem("r3_ready")
        x2_ready = sem("x2_ready")
        xt_ps = sem("xt_ps")
        xt_hi = sem("xt_hi")
        xt_lo = sem("xt_lo")
        stored = [sem("stored0"), sem("stored1")]
        stage_free = [sem("stage_free0"), sem("stage_free1")]
        w_in_sem = sem("w_landed")
        q_abs = sem("q_abs")
        q_norm = sem("q_norm")
        q_rounded = sem("q_rounded")
        q_int_ready = sem("q_int_ready")
        q_dif_ready = sem("q_dif_ready")
        q_sq_ready = sem("q_sq_ready")
        q_deq = sem("q_deq")
        w_q_ready = sem("w_q_ready")
        w_t_ps = sem("w_t_ps")
        w_hi_ready = sem("w_hi_ready")
        w_lo_ready = sem("w_lo_ready")
        dve_step = sem("dve_step")
        pool_step = sem("pool_step")
        dve_pro = sem("dve_pro")
        pool_pro = sem("pool_pro")
        x_in = [sem("x_in0"), sem("x_in1")]
        acc_in = [sem("acc_in0"), sem("acc_in1")]
        r3_part = sem("r3_part")
        quad_done = sem("quad_done")
        drive_done = sem("drive_done")
        scan_done = sem("scan_done")
        bn_done = sem("bn_done")
        acc_out = [sem("acc_out0"), sem("acc_out1")]
        z_ps = sem("z_ps")
        relu_ready = sem("relu_ready")
        g_ready = sem("g_ready")
        g_hi_ready = sem("g_hi_ready")
        g_lo_ready = sem("g_lo_ready")
        o_ps = sem("o_ps")
        o_added = sem("o_added")

        def blocks(ap):
            return ap.rearrange("p (b e) -> p b e", e=QB)

        def per_block(ap):
            return ap.unsqueeze(2).to_broadcast([P, NB, QB])

        def w_load(eng, u):
            eng.dma_start(w_raw[:, 0:HALF], w_fc[bass.ds(u, 1), :, :].rearrange("a p n -> p (a n)")).then_inc(w_in_sem, 16)
            eng.dma_start(w_raw[:, HALF:UW], w_proj[bass.ds(u, 1), :, :].rearrange("a p n -> p (a n)")).then_inc(w_in_sem, 16)

        def act_abs(act, u):
            act.wait_ge(w_in_sem, u * 32 + 32)
            act.activation(w_abs[:], w_raw[:], ACT.Abs).then_inc(q_abs, 1)

        def act_round(act, u, s):
            if s == 0:
                act.wait_ge(q_norm, u + 1)
            if s >= RING:
                act.wait_ge(q_int_ready, u * NS + s - RING + 1)
            act.activation(q_mag[:, s % RING, :], w_norm[:], ACT.Identity, bias=magic[:, 0:1],
                           scale=1.0 / SHRINKS[s]).then_inc(q_rounded, 1)

        def act_square(act, u, s):
            act.wait_ge(q_dif_ready, u * NS + s + 1)
            act.activation(q_sq[:, s % RING, :], q_dif[:, s % RING, :], ACT.Square).then_inc(q_sq_ready, 1)

        def act_shrink(act, u, s):
            if s < NS:
                act_round(act, u, s)
            if 2 <= s < NS + 2:
                act_square(act, u, s - 2)

        def act_weights(act, u):
            act.wait_ge(w_t_ps, u + 1)
            act.activation(w_hi[:, bass.ds(u, 1), :].rearrange("p a n -> p (a n)"), bank[Q_BANK][:], ACT.Copy).then_inc(w_hi_ready, 1)

        def dve_link(dve, ins, base, n):
            ins.then_inc(dve_step, 1)
            dve.wait_ge(dve_step, base + n)

        UNIT_STEPS = 14

        def dve_norm(dve, u, base):
            dve.wait_ge(w_in_sem, u * 32 + 32)
            dve_link(dve, dve.tensor_reduce(qs[:, 0, :], blocks(w_raw[:]), AX, ALU.max, apply_absolute_value=True), base, 1)
            dve_link(dve, dve.tensor_scalar(qs[:, 1, :], qs[:, 0, :], 1e-8, 1.0 / QMAX, ALU.max, ALU.mult), base, 2)
            dve_link(dve, dve.reciprocal(qs[:, 2, :], qs[:, 1, :]), base, 3)
            dve.wait_ge(q_abs, u + 1)
            dve.tensor_tensor(blocks(w_norm[:]), blocks(w_abs[:]), per_block(qs[:, 2, :]), ALU.mult).then_inc(q_norm, 1)

        def dve_shrink(dve, u, s):
            if s < NS:
                dve.wait_ge(q_rounded, u * NS + s + 1)
                dve.tensor_scalar(q_int[:, s % RING, :], q_mag[:, s % RING, :], MAGIC + QMAX, MAGIC, ALU.min,
                                  ALU.subtract).then_inc(q_int_ready, 1)
            if 1 <= s < NS + 1:
                r = s - 1
                dve.wait_ge(q_int_ready, u * NS + r + 1)
                if r >= RING:
                    dve.wait_ge(q_sq_ready, u * NS + r - RING + 1)
                dve.scalar_tensor_tensor(out=q_dif[:, r % RING, :], in0=q_int[:, r % RING, :], scalar=SHRINKS[r],
                                         in1=w_norm[:], op0=ALU.mult, op1=ALU.subtract).then_inc(q_dif_ready, 1)
            if 2 <= s < NS + 2:
                r = s - 2
                dve.wait_ge(q_sq_ready, u * NS + r + 1)
                dve.tensor_reduce(err[:, r, :], blocks(q_sq[:, r % RING, :]), AX, ALU.add).then_inc(dve_step, 1) if r == NS - 1 \
                    else dve.tensor_reduce(err[:, r, :], blocks(q_sq[:, r % RING, :]), AX, ALU.add)

        def dve_select(dve, u, base):
            by_block = err[:].rearrange("p s b -> p b s")
            dve.wait_ge(dve_step, base + 4)
            dve_link(dve, dve.tensor_reduce(qs[:, 3, :], by_block, AX, ALU.min), base, 5)
            least = qs[:, 3, :].unsqueeze(1).to_broadcast([P, NS, NB])
            rank = shrink_rank[:].unsqueeze(2).to_broadcast([P, NS, NB])
            value = shrink_val[:].unsqueeze(2).to_broadcast([P, NS, NB])
            dve_link(dve, dve.tensor_tensor(pick[:, 0, :, :], err[:], least, ALU.is_equal), base, 6)
            dve_link(dve, dve.tensor_tensor(pick[:, 1, :, :], pick[:, 0, :, :], rank, ALU.mult), base, 7)
            dve_link(dve, dve.tensor_reduce(qs[:, 4, :], pick[:, 1, :, :].rearrange("p s b -> p b s"), AX, ALU.max), base, 8)
            first = qs[:, 4, :].unsqueeze(1).to_broadcast([P, NS, NB])
            dve_link(dve, dve.tensor_tensor(pick[:, 0, :, :], pick[:, 1, :, :], first, ALU.is_equal), base, 9)
            dve_link(dve, dve.tensor_tensor(pick[:, 1, :, :], pick[:, 0, :, :], value, ALU.mult), base, 10)
            dve_link(dve, dve.tensor_reduce(qs[:, 5, :], pick[:, 1, :, :].rearrange("p s b -> p b s"), AX, ALU.max), base, 11)
            dve_link(dve, dve.tensor_tensor(qs[:, 6, :], qs[:, 5, :], qs[:, 1, :], ALU.mult), base, 12)
            dve_link(dve, dve.reciprocal(qs[:, 7, :], qs[:, 6, :]), base, 13)
            dve_link(dve, dve.tensor_tensor(blocks(w_abs[:]), blocks(w_raw[:]), per_block(qs[:, 7, :]), ALU.mult), base, 14)

        FINAL_STEPS = 2

        def dve_dequant(dve, u, base):
            dve_link(dve, dve.tensor_scalar(w_norm[:], w_abs[:], MAGIC, MAGIC + QMAX, ALU.add, ALU.min), base, 15)
            dve_link(dve, dve.tensor_scalar(w_abs[:], w_norm[:], MAGIC - QMAX, MAGIC, ALU.max, ALU.subtract), base, 16)
            dve.tensor_tensor(blocks(w_norm[:]), blocks(w_abs[:]), per_block(qs[:, 6, :]), ALU.mult).then_inc(q_deq, 1)

        QSTEPS = UNIT_STEPS + FINAL_STEPS

        def dve_weights(dve, u):
            dve.wait_ge(w_hi_ready, u + 1)
            hi = w_hi[:, bass.ds(u, 1), :].rearrange("p a n -> p (a n)")
            lo = w_lo[:, bass.ds(u, 1), :].rearrange("p a n -> p (a n)")
            dve.tensor_tensor(lo, bank[Q_BANK][:], hi, ALU.subtract).then_inc(w_lo_ready, 1)

        def pool_link(pool, ins, base, n):
            ins.then_inc(pool_step, 1)
            pool.wait_ge(pool_step, base + n)

        def pool_straight(pool, u, base, n):
            pool.wait_ge(q_deq, u + 1)
            pool_link(pool, pool.tensor_tensor(w_norm[:], w_norm[:], w_raw[:], ALU.subtract), base, n)
            pool.tensor_tensor(w_q[:], w_raw[:], w_norm[:], ALU.add).then_inc(w_q_ready, 1)

        def pe_weights(pe, u):
            pe.wait_ge(w_q_ready, u + 1)
            for k in range(UT):
                last = pe.transpose(bank[Q_BANK][:, k * P:(k + 1) * P], w_q[:, k * P:(k + 1) * P], ident[:])
            last.then_inc(w_t_ps, 1)

        block = ctx.enter_context(nc.Block())

        @block.sync
        def _(sp):
            sp.dma_start(idx[:], ids).then_inc(idx_in, 16)
            w_load(sp, 0)
            w_in_v = w_in.rearrange("(k p) n -> p k n", p=P)
            w_skip_v = w_skip.rearrange("(k p) n -> p k n", p=P)
            sp.dma_start(wc[:, :, 0:GATES], w_in_v).then_inc(consts_in, 16)
            sp.dma_start(wc[:, :, GATES:GATES + D], w_skip_v).then_inc(consts_in, 16)
            sp.dma_start(gamma_sb[:], gamma).then_inc(consts_in, 16)
            sp.dma_start(beta_sb[:], beta).then_inc(consts_in, 16)
            sp.dma_start(b_in_sb[:], b_in).then_inc(consts_in, 16)
            sp.dma_start(w_out_sb[:], w_out).then_inc(consts_in, 16)
            sp.dma_start(bias_bc[:], b_out.partition_broadcast(P)).then_inc(consts_in, 16)
            sp.dma_start(quad[:].rearrange("p a b -> p (a b)"), b_skip.partition_broadcast(P)).then_inc(consts_in, 16)

            with sp.Fori(0, PAIRS) as i:
                for e in range(2):
                    sp.wait_ge(xt_hi, i * 2 * KD + (e + 1) * KD)
                    sp.wait_ge(xt_lo, i * 2 * KD + (e + 1) * KD)
                    sp.dma_start(xt_dram[bass.ds(i * 2 + e, 1), :, :].rearrange("a p n -> p (a n)"),
                                 xt[:, e].rearrange("p a k t -> p (a k t)")).then_inc(stored[e], 16)
                    sp.dma_start(acc_dram[bass.ds(i * 2 + e, 1), :, :].rearrange("a p n -> p (a n)"),
                                 res[:, e].rearrange("p k d -> p (k d)")).then_inc(stored[e], 16)
                for e in range(2):
                    sp.wait_ge(stored[e], i * 32 + 32)
                    sp.nop().then_inc(stage_free[e], 1)

            def load_x(g, e):
                sp.dma_start(xt[:, e].rearrange("p a k t -> p (a k t)"),
                             xt_dram[bass.ds(g, 1), :, :].rearrange("a p n -> p (a n)")).then_inc(x_in[e], 16)

            def load_acc(g, e):
                sp.dma_start(res[:, e].rearrange("p k d -> p (k d)"),
                             acc_dram[bass.ds(g, 1), :, :].rearrange("a p n -> p (a n)")).then_inc(acc_in[e], 16)

            def after_group(n, g, g_next, e, to_out):
                if g_next is not None:
                    sp.wait_ge(z_ps, n * 2 * HC + (e + 1) * HC)
                    load_x(g_next, e)
                sp.wait_ge(o_added, n * 2 * KT + KT * (e + 1) + KT)
                if to_out:
                    sp.dma_start(out[bass.ds(g, 1), :, :].rearrange("a (k p) d -> p (a k) d", p=P),
                                 res[:, e]).then_inc(acc_out[e], 16)
                else:
                    sp.dma_start(acc_dram[bass.ds(g, 1), :, :].rearrange("a p n -> p (a n)"),
                                 res[:, e].rearrange("p k d -> p (k d)")).then_inc(acc_out[e], 16)
                sp.wait_ge(acc_out[e], n * 16 + 16)
                if g_next is not None:
                    load_acc(g_next, e)

            for e in range(2):
                load_x(e, e)
                load_acc(e, e)
            for ph in range(PHASES):
                last_phase = ph == PHASES - 1
                with sp.Fori(0, PAIRS - 1) as i:
                    for e in range(2):
                        after_group(i + ph * PAIRS, i * 2 + e, i * 2 + 2 + e, e, last_phase)
                for e in range(2):
                    after_group(ph * PAIRS + PAIRS - 1, SEQS - 2 + e, e if ph < PHASES - 1 else None, e, last_phase)

        @block.gpsimd
        def _(pool):
            pool.memset(ident[:], 0.0).then_inc(pool_pro, 1)
            pool.wait_ge(pool_pro, 1)
            pool.affine_select(out=ident[:], in_=ident[:], compare_op=ALU.not_equal, fill=1.0, base=0,
                               pattern=[[-1, P]], channel_multiplier=1).then_inc(pool_const, 1)
            pool.memset(ones_mean[:], 1.0 / TOK).then_inc(pool_const, 1)
            pool.memset(magic[:], MAGIC).then_inc(pool_const, 1)
            for s in range(NS):
                pool.memset(shrink_val[:, s:s + 1], SHRINKS[s])
                pool.memset(shrink_rank[:, s:s + 1], float(NS - s)).then_inc(pool_const, 1)
            pool.memset(eps[:], EPS)
            pool.memset(neg_one[:], -1.0)
            pool.memset(neg_half[:], -0.5).then_inc(pool_pro, 1)
            pool.wait_ge(pool_pro, 2)

            def gather(i):
                pool.tensor_copy(idx_now[:], idx[:, bass.ds(i * 2 * KT, 2 * KT)]).then_inc(idx_ready, 1)
                pool.wait_ge(idx_ready, i + 1)
                pool.tensor_tensor(idx_seen[:], neg_one[:, 0:1], neg_one[:, 0:1], ALU.mult)
                for k in range(2 * KT):
                    pool.indirect_dma_start(emb_next[:, k, :], None, table,
                                            bass.IndirectOffsetOnAxis(ap=idx_now[:, k:k + 1], axis=0)).then_inc(emb_in, 16)

            POOL_STEPS = 6 + 2 * 2 + 1

            def rsqrt_pair(i):
                base = i * POOL_STEPS
                pool.wait_ge(var1_ready, i + 1)
                pool_link(pool, pool.tensor_tensor(stat[:, 0, :], var1[:], eps[:], ALU.add), base, 1)
                pool_link(pool, pool.tensor_tensor(stat[:, 1, :], stat[:, 0, :], neg_half[:], ALU.pow), base, 2)
                pool_link(pool, pool.tensor_tensor(stat[:, 2, :], var1[:], stat[:, 1, :], ALU.mult), base, 3)
                pool_link(pool, pool.tensor_tensor(stat[:, 3, :], stat[:, 2, :], stat[:, 1, :], ALU.mult), base, 4)
                pool_link(pool, pool.tensor_tensor(stat[:, 4, :], stat[:, 3, :], eps[:], ALU.add), base, 5)
                pool_link(pool, pool.tensor_tensor(stat[:, 5, :], stat[:, 4, :], neg_half[:], ALU.pow), base, 6)
                pool.tensor_tensor(stat[:, 6, :], stat[:, 5, :], stat[:, 1, :], ALU.mult).then_inc(r12_ready, 1)

            def rsqrt_mlp(i, e):
                base = i * POOL_STEPS + 6 + 2 * e
                pool.wait_ge(mv_ready, i * 2 + e + 1)
                mv = mean_var[:, e * KT:(e + 1) * KT, :]
                pool_link(pool, pool.tensor_tensor(stat3[:, e, 0, :], mv[:, :, 1], eps[:, 0:KT], ALU.add), base, 1)
                pool_link(pool, pool.tensor_tensor(stat3[:, e, 1, :], stat3[:, e, 0, :], neg_half[:, 0:KT], ALU.pow), base, 2)
                pool.tensor_tensor(stat3[:, e, 2, :], mv[:, :, 0], neg_one[:], ALU.mult).then_inc(r3_part, 1)
                pool.wait_ge(r3_part, i * 2 + e + 1)
                pool.tensor_tensor(stat3[:, e, 3, :], stat3[:, e, 2, :], stat3[:, e, 1, :], ALU.mult).then_inc(r3_ready, 1)

            pool.wait_ge(idx_in, 16)
            gather(0)

            def mixer_step(i, more):
                if more:
                    pool.wait_ge(emb2_ready, i + 1)
                    pool.wait_ge(emb_in, i * 2 * KT * 16 + 2 * KT * 16)
                    gather(i + 1)
                rsqrt_pair(i)
                rsqrt_mlp(i, 0)
                rsqrt_mlp(i, 1)
                pool_straight(pool, i, i * POOL_STEPS, POOL_STEPS)

            with pool.Fori(0, PAIRS - 1) as i:
                mixer_step(i, True)
            mixer_step(PAIRS - 1, False)

            def low_part(n, k):
                pool.wait_ge(g_ready, n * 2 * HC + k + 1)
                pool.wait_ge(g_hi_ready, n * 2 * HC + k + 1)
                pool.tensor_tensor(g_lo[:, k % 2, :], act_g[:, k % 2, :], g_hi[:, k % 2, :], ALU.subtract).then_inc(g_lo_ready, 1)

            for ph in range(PHASES):
                with pool.Fori(0, PAIRS) as i:
                    n = i + ph * PAIRS
                    for k in range(2 * HC):
                        low_part(n, k)
                    if ph < PHASES - 1:
                        pool_straight(pool, n + PAIRS, n + PAIRS * POOL_STEPS, 1)

        @block.tensor
        def _(pe):
            pe.wait_ge(consts_in, 8 * 16)
            pe.wait_ge(pool_const, 3 + NS)
            for j in range(3):
                for k in range(KD):
                    last = pe.matmul(bank[0][:, j:j + 1], wc[:, k, j * S:(j + 1) * S], beta_sb[:, k:k + 1],
                                     start=(k == 0), stop=(k == KD - 1))
            last.then_inc(cin_ps, 1)
            pe.wait_ge(wg_ready, 1)
            for k in range(KD):
                pe.matmul(bank[1][:, 0:GATES], ones_mean[:], wc[:, k, 0:GATES], start=(k == 0), stop=(k == KD - 1))
            for k in range(KD):
                last = pe.matmul(bank[2][:], ones_mean[:], wc[:, k, GATES:GATES + D], start=(k == 0), stop=(k == KD - 1))
            last.then_inc(wmean_ps, 1)
            pe.wait_ge(wc_ready, 1)
            pe.wait_ge(zero_gate, 1)

            def emb_of(e, k):
                return emb2[:, e * KT + k, 0, :]

            with pe.Fori(0, PAIRS) as i:
                pe.wait_ge(emb2_ready, i + 1)
                for e in range(2):
                    for k in range(KT):
                        last = pe.matmul(bank[0][:, e * EMB:(e + 1) * EMB], ones_mean[:], emb_of(e, k),
                                         start=(k == 0), stop=(k == KT - 1))
                last.then_inc(mean_ps, 1)
                for e in range(2):
                    for k in range(KT):
                        last = pe.transpose(bank[2 + e][0:EMB, k * P:(k + 1) * P], emb_of(e, k), ident[:])
                    last.then_inc(et_ps, 1)

                def project(e):
                    ba, bb = PROJ_BANK[e]
                    for k in range(KT):
                        both = emb2[:, e * KT + k, :, :].rearrange("p a b -> p (a b)")
                        pe.matmul(bank[ba][:, 0:GATES], both, wc[:, k, 0:GATES], start=(k == 0), stop=(k == KT - 1))
                        last = pe.matmul(bank[bb][:], both, wc[:, k, GATES:GATES + D], start=(k == 0), stop=(k == KT - 1))
                    last.then_inc(proj_ps, 1)

                project(0)
                pe.wait_ge(emb_c_ready, i + 1)
                for e in range(2):
                    for k in range(KT):
                        last = pe.matmul(bank[0][0:EMB, P + e * EMB:P + (e + 1) * EMB], emb_c[:, e * KT + k, :],
                                         emb_c[:, e * KT + k, :], start=(k == 0), stop=(k == KT - 1))
                last.then_inc(cov_ps, 1)
                pe.wait_ge(et_sb, 2 * i + 2)
                pe.wait_ge(cov_sb, i + 1)
                for e in range(2):
                    for k in range(KT):
                        m = e * KT + k
                        last = pe.matmul(bank[1][:, m * EMB:(m + 1) * EMB], lhs[0:EMB, e, k * P:(k + 1) * P],
                                         cov[:, e, :], start=True, stop=True)
                last.then_inc(quad_ps, 1)
                project(1)
                pe.wait_ge(scaled_ready, i + 1)
                for e in range(2):
                    for k in range(KT):
                        last = pe.transpose(bank[2 + e][:, k * P:(k + 1) * P],
                                            scaled[:, e * KT + k, :, :].rearrange("p a b -> p (a b)"), ident[:])
                    last.then_inc(scaled_ps, 1)
                for e in range(2):
                    pe.wait_ge(gate_x_ready, 2 * i + e + 1)
                    pe.wait_ge(gate_w_ready, 2 * i + 2)
                    pe.wait_ge(skip_ready, 2 * i + 2)
                    if e == 1:
                        pe.wait_ge(gate_x_ready, 2 * i + 2)
                    for j in range(3):
                        b = GATE_BANK[e][j]
                        pe.matmul(bank[b][:], gate_w[:, e, j * S:(j + 1) * S], gate_x[:, e, :],
                                  start=True, stop=True).then_inc(gates_ps, 1)
                for e in range(2):
                    pe.wait_ge(y_ready, 2 * i + e + 1)
                    for k in range(KT):
                        m = e * KT + k
                        if m == 7:
                            pe.wait_ge(h2_sb, 2 * KT * i + 1)
                        pe.matmul(bank[H2_BANK[m]][:], lhs[:, e, k * P:(k + 1) * P], rhs[:, e, :], start=True, stop=False)
                        pe.matmul(bank[H2_BANK[m]][:], gate_y[:, e, k * P:(k + 1) * P], w_out_sb[:],
                                  start=False, stop=True).then_inc(h2_ps, 1)
                for e in range(2):
                    pe.wait_ge(x2_ready, 2 * i + e + 1)
                    pe.wait_ge(h2_sb, 2 * KT * i + (6, 8)[e])
                    for d in range(KD):
                        m = e * KD + d
                        if m == 7:
                            pe.wait_ge(xt_lo, 2 * KD * i + 1)
                        for k in range(KT):
                            last = pe.transpose(bank[XT_BANK[m]][:, k * P:(k + 1) * P], mix[:, e, k, d * P:(d + 1) * P], ident[:])
                        last.then_inc(xt_ps, 1)
                pe_weights(pe, i)

            def mlp_step(ph, n):
                unit0 = ph * PAIRS

                def up(e, c):
                    z = bank[c % 2][:]
                    for d in range(KD):
                        u, t = unit0 + 2 * c + d // 2, d % 2
                        hi, lo = w_hi[:, u, t * P:(t + 1) * P], w_lo[:, u, t * P:(t + 1) * P]
                        pe.matmul(z, hi, xt[:, e, 0, d, :], start=(d == 0), stop=False)
                        pe.matmul(z, hi, xt[:, e, 1, d, :], start=False, stop=False)
                        last = pe.matmul(z, lo, xt[:, e, 0, d, :], start=False, stop=(d == KD - 1))
                    last.then_inc(z_ps, 1)

                def down(e, c):
                    pe.wait_ge(g_hi_ready, n * 2 * HC + e * HC + c + 1)
                    pe.wait_ge(g_lo_ready, n * 2 * HC + e * HC + c + 1)
                    t = 2 + c % 2
                    sel = slice(unit0 + c // 2, unit0 + 8, 2)
                    w_h, w_l = w_hi[:, sel, t * P:(t + 1) * P], w_lo[:, sel, t * P:(t + 1) * P]
                    for k in range(KT):
                        o = bank[2 + k][:].rearrange("p (a b) -> p a b", b=P)
                        if c == 0:
                            pe.wait_ge(o_added, n * 2 * KT + e * KT + k + 1)
                        ghi, glo = g_hi[:, c % 2, k * P:(k + 1) * P], g_lo[:, c % 2, k * P:(k + 1) * P]
                        pe.matmul(o, ghi, w_h, start=(c == 0), stop=False)
                        pe.matmul(o, ghi, w_l, start=False, stop=False)
                        last = pe.matmul(o, glo, w_h, start=False, stop=(c == HC - 1))
                        if c == HC - 1:
                            last.then_inc(o_ps, 1)

                for e in range(2):
                    pe.wait_ge(x_in[e], n * 16 + 16)
                    up(e, 0)
                    for c in range(1, HC):
                        up(e, c)
                        down(e, c - 1)
                    down(e, HC - 1)

            for ph in range(PHASES):
                pe.wait_ge(w_hi_ready, (ph + 1) * PAIRS)
                pe.wait_ge(w_lo_ready, (ph + 1) * PAIRS)
                with pe.Fori(0, PAIRS) as i:
                    mlp_step(ph, i + ph * PAIRS)
                    if ph < PHASES - 1:
                        pe_weights(pe, i + (ph + 1) * PAIRS)

        @block.scalar
        def _(act):
            for e in range(2):
                act.nop().then_inc(stage_free[e], 1)
            act.wait_ge(pool_const, 3 + NS)
            act.wait_ge(cin_ready, 1)
            with act.Fori(0, PAIRS) as i:
                act_abs(act, i)
                for e in range(2):
                    act.wait_ge(et_ps, 2 * i + e + 1)
                    act.activation(lhs[0:EMB, e, :], bank[2 + e][0:EMB, :], ACT.Copy)
                    act.activation(rhs[0:EMB, e, :], bank[2 + e][0:EMB, :], ACT.Copy, scale=0.125).then_inc(et_sb, 1)
                act_shrink(act, i, 0)
                act_shrink(act, i, 1)
                act.wait_ge(cov_ps, i + 1)
                act.activation(cov[:].rearrange("p a b -> p (a b)"), bank[0][0:EMB, P:2 * P], ACT.Copy,
                               scale=1.0 / (EMB * D)).then_inc(cov_sb, 1)
                act_shrink(act, i, 2)
                act_shrink(act, i, 3)
                for e in range(2):
                    act.wait_ge(proj_ps, 2 * i + e + 1)
                    ba, bb = PROJ_BANK[e]
                    act.activation(gate_w[0:EMB, e, :], bank[ba][0:EMB, 0:GATES], ACT.Copy, scale=0.125).then_inc(gate_w_ready, 1)
                    act.activation(rhs[EMB:P, e, :], bank[bb][EMB:P, :], ACT.Copy, scale=0.125).then_inc(skip_ready, 1)
                    act_shrink(act, i, 4 + e)
                act_shrink(act, i, 6)
                act_shrink(act, i, 7)
                for e in range(2):
                    act.wait_ge(scaled_ps, 2 * i + e + 1)
                    act.activation(gate_x[:, e, :], bank[2 + e][:], ACT.Copy)
                    act.activation(lhs[EMB:P, e, :], bank[2 + e][EMB:P, :], ACT.Copy).then_inc(gate_x_ready, 1)
                act_shrink(act, i, 8)
                for e in range(2):
                    b0, _, b2 = GATE_BANK[e]
                    act.wait_ge(gates_ps, 6 * i + 3 * e + 3)
                    act.activation(mix[:, e, 0, :], bank[b0][:], ACT.Sigmoid, bias=c_in[:, 0:1]).then_inc(alpha_ready, 1)
                    act.activation(gate_y[:, e, :], bank[b2][:], ACT.Tanh, bias=c_in[:, 2:3]).then_inc(tanh_ready, 1)
                    act_shrink(act, i, 9 + e)
                act_shrink(act, i, 11)
                act_shrink(act, i, 12)
                act_shrink(act, i, 13)
                for e in range(2):
                    act.wait_ge(r3_ready, 2 * i + e + 1)
                    for k in range(KT):
                        last = act.activation(mix[:, e, k, :], res[:, e, k, :], ACT.Identity, bias=stat3[:, e, 3, k:k + 1],
                                              scale=stat3[:, e, 1, k:k + 1])
                    last.then_inc(x2_ready, 1)
                    act_shrink(act, i, 14 + e)
                for e in range(2):
                    act.wait_ge(stage_free[e], i + 1)
                    for d in range(KD):
                        m = e * KD + d
                        act.wait_ge(xt_ps, 2 * KD * i + m + 1)
                        act.activation(xt[:, e, 0, d, :], bank[XT_BANK[m]][:], ACT.Copy).then_inc(xt_hi, 1)
                    act_shrink(act, i, 16 + e)
                act_weights(act, i)
                w_load(act, i + 1)

            def mlp_step(n, quant):
                if quant:
                    act_abs(act, n + PAIRS)
                for k in range(2 * HC):
                    act.wait_ge(z_ps, n * 2 * HC + k + 1)
                    act.activation(relu_z[:, k % 2, :], bank[k % 2][:], ACT.Relu).then_inc(relu_ready, 1)
                    act.wait_ge(relu_ready, n * 2 * HC + k + 1)
                    act.activation(g_hi[:, k % 2, :], relu_z[:, k % 2, :], ACT.Square).then_inc(g_hi_ready, 1)
                    if quant:
                        act_shrink(act, n + PAIRS, 2 * k)
                        act_shrink(act, n + PAIRS, 2 * k + 1)
                if quant:
                    act_shrink(act, n + PAIRS, NS)
                    act_shrink(act, n + PAIRS, NS + 1)
                    act_weights(act, n + PAIRS)

            for ph in range(PHASES - 1):
                if ph < PHASES - 2:
                    with act.Fori(0, PAIRS) as i:
                        mlp_step(i + ph * PAIRS, True)
                        w_load(act, i + (ph + 1) * PAIRS + 1)
                else:
                    with act.Fori(0, PAIRS - 1) as i:
                        mlp_step(i + ph * PAIRS, True)
                        w_load(act, i + (ph + 1) * PAIRS + 1)
                    mlp_step(ph * PAIRS + PAIRS - 1, True)
            with act.Fori(0, PAIRS) as i:
                mlp_step(i + (PHASES - 1) * PAIRS, False)

        @block.vector
        def _(dve):
            dve.memset(gate_w[EMB:P, :, :], 0.0).then_inc(zero_gate, 1)
            dve.wait_ge(consts_in, 8 * 16)
            dve.tensor_tensor(bias_bc[:], bias_bc[:], quad[:].rearrange("p a b -> p (a b)"), ALU.add).then_inc(bias_done, 1)
            dve.wait_ge(cin_ps, 1)
            dve.tensor_tensor(c_in[:], bank[0][:, 0:3], b_in_sb[:], ALU.add).then_inc(cin_ready, 1)
            for k in range(KD):
                last = dve.tensor_scalar(wc[:, k, 0:GATES], wc[:, k, 0:GATES], gamma_sb[:, k:k + 1], None, ALU.mult)
            last.then_inc(wg_ready, 1)
            dve.wait_ge(wg_ready, 1)
            dve.wait_ge(wmean_ps, 1)
            for k in range(KD):
                dve.tensor_tensor(wc[:, k, 0:GATES], wc[:, k, 0:GATES], bank[1][:, 0:GATES], ALU.subtract)
                last = dve.tensor_tensor(wc[:, k, GATES:GATES + D], wc[:, k, GATES:GATES + D], bank[2][:], ALU.subtract)
            last.then_inc(wc_ready, 1)
            dve.wait_ge(bias_done, 1)
            dve.wait_ge(pool_const, 3 + NS)
            dve.memset(bn6[:, 0, 0:1], 0.0).then_inc(o_added, KT)

            with dve.Fori(0, PAIRS) as i:
                base = i * QSTEPS
                dve.wait_ge(emb_in, i * 2 * KT * 16 + 2 * KT * 16)
                dve.tensor_copy(emb2[:], emb_next[:].unsqueeze(2).to_broadcast([P, 2 * KT, 2, EMB])).then_inc(emb2_ready, 1)
                dve_norm(dve, i, base)
                dve.wait_ge(emb2_ready, i + 1)
                dve.wait_ge(mean_ps, i + 1)
                for e in range(2):
                    mean = bank[0][:, e * EMB:(e + 1) * EMB].unsqueeze(1).to_broadcast([P, KT, EMB])
                    last = dve.tensor_tensor(emb_c[:, e * KT:(e + 1) * KT, :], emb2[:, e * KT:(e + 1) * KT, 0, :], mean, ALU.subtract)
                last.then_inc(emb_c_ready, 1)
                for s in range(0, 4):
                    dve_shrink(dve, i, s)
                dve.wait_ge(quad_ps, i + 1)
                dve.tensor_tensor(quad[:], bank[1][:].rearrange("p (a b) -> p a b", b=EMB), emb2[:, :, 0, :],
                                  ALU.mult).then_inc(quad_done, 1)
                dve.wait_ge(quad_done, i + 1)
                dve.tensor_reduce(var1[:], quad[:], AX, ALU.add).then_inc(var1_ready, 1)
                for s in range(4, 8):
                    dve_shrink(dve, i, s)
                dve.wait_ge(r12_ready, i + 1)
                dve.tensor_tensor(scaled[:, :, 0, :], emb2[:, :, 0, :], stat[:, 6, :].unsqueeze(2).to_broadcast([P, 2 * KT, EMB]), ALU.mult)
                dve.tensor_tensor(scaled[:, :, 1, :], emb2[:, :, 0, :], stat[:, 1, :].unsqueeze(2).to_broadcast([P, 2 * KT, EMB]),
                                  ALU.mult).then_inc(scaled_ready, 1)
                dve_shrink(dve, i, 8)
                for e in range(2):
                    b1 = GATE_BANK[e][1]
                    alpha, keep, drive, state = (mix[:, e, j, :] for j in range(4))
                    dve.wait_ge(alpha_ready, 2 * i + e + 1)
                    dve.tensor_scalar(keep, alpha, -1.0, 1.0, ALU.mult, ALU.add)
                    dve.scalar_tensor_tensor(out=drive, in0=bank[b1][:], scalar=c_in[:, 1:2], in1=alpha, op0=ALU.add,
                                             op1=ALU.mult).then_inc(drive_done, 1)
                    dve_shrink(dve, i, 9 + e)
                    dve.wait_ge(drive_done, 2 * i + e + 1)
                    dve.tensor_tensor_scan(state, keep, drive, 0.0, ALU.mult, ALU.add).then_inc(scan_done, 1)
                    dve.wait_ge(scan_done, 2 * i + e + 1)
                    dve.wait_ge(tanh_ready, 2 * i + e + 1)
                    dve.tensor_tensor(gate_y[:, e, :], state, gate_y[:, e, :], ALU.mult).then_inc(y_ready, 1)
                dve_shrink(dve, i, 11)
                for e in range(2):
                    dve.wait_ge(stage_free[e], i + 1)
                    for k in range(KT):
                        m = e * KT + k
                        dve.wait_ge(h2_ps, 2 * KT * i + m + 1)
                        dve.tensor_tensor(res[:, e, k, :], bank[H2_BANK[m]][:], bias_bc[:], ALU.add).then_inc(h2_sb, 1)
                        if k >= 1:
                            dve.wait_ge(h2_sb, 2 * KT * i + m)
                            dve.bn_stats(bn6[:, m - 1, :], res[:, e, k - 1, :])
                    dve.wait_ge(h2_sb, 2 * KT * i + (e + 1) * KT)
                    dve.bn_stats(bn6[:, e * KT + KT - 1, :], res[:, e, KT - 1, :]).then_inc(bn_done, 1)
                    dve.wait_ge(bn_done, 2 * i + e + 1)
                    dve_shrink(dve, i, 12 + e)
                    for k in range(KT):
                        last = dve.bn_aggr(mean_var[:, e * KT + k, :], bn6[:, e * KT + k, :])
                    last.then_inc(mv_ready, 1)
                dve_shrink(dve, i, 14)
                dve_shrink(dve, i, 15)
                for e in range(2):
                    for d in range(KD):
                        m = e * KD + d
                        dve.wait_ge(xt_hi, 2 * KD * i + m + 1)
                        dve.tensor_tensor(xt[:, e, 1, d, :], bank[XT_BANK[m]][:], xt[:, e, 0, d, :],
                                          ALU.subtract).then_inc(xt_lo, 1)
                    dve_shrink(dve, i, 16 + e)
                dve_select(dve, i, base)
                dve_dequant(dve, i, base)
                dve_weights(dve, i)

            def add_group(n, e):
                dve.wait_ge(acc_in[e], n * 16 + 16)
                for k in range(KT):
                    dve.wait_ge(o_ps, n * 2 * KT + e * KT + k + 1)
                    dve.tensor_tensor(res[:, e, k, :], bank[2 + k][:], res[:, e, k, :], ALU.add).then_inc(o_added, 1)

            def mlp_step(n, quant):
                u = n + PAIRS
                base = u * QSTEPS
                if quant:
                    dve_norm(dve, u, base)
                for k in range(2 * HC):
                    dve.wait_ge(relu_ready, n * 2 * HC + k + 1)
                    dve.scalar_tensor_tensor(out=act_g[:, k % 2, :], in0=bank[k % 2][:], scalar=0.0, in1=relu_z[:, k % 2, :],
                                             op0=ALU.max, op1=ALU.mult).then_inc(g_ready, 1)
                    if quant:
                        dve_shrink(dve, u, 2 * k)
                        dve_shrink(dve, u, 2 * k + 1)
                    if k == HC:
                        add_group(n, 0)
                if quant:
                    dve_shrink(dve, u, NS)
                    dve_shrink(dve, u, NS + 1)
                    dve_select(dve, u, base)
                    dve_dequant(dve, u, base)
                add_group(n, 1)
                if quant:
                    dve_weights(dve, u)

            for ph in range(PHASES):
                with dve.Fori(0, PAIRS) as i:
                    mlp_step(i + ph * PAIRS, ph < PHASES - 1)


def kernel(x, L0_tok_weight, L0_attn_gamma, L0_attn_beta, L0_attn_W_in, L0_attn_b_in, L0_attn_W_out, L0_attn_b_out,
           L0_attn_W_skip, L0_attn_b_skip, L0_ffn_w_fc, L0_ffn_w_proj):
    import concourse.bacc as bacc
    from concourse.bass_utils import run_bass_kernel_spmd

    arr = np.asarray
    halves = D // HALF
    arrays = {
        "ids": arr(x).reshape(SEQS * KT, P).T,
        "table": arr(L0_tok_weight),
        "gamma": arr(L0_attn_gamma).reshape(KD, P).T,
        "beta": arr(L0_attn_beta).reshape(KD, P).T,
        "w_in": arr(L0_attn_W_in),
        "b_in": arr(L0_attn_b_in).reshape(3, S).T,
        "w_out": arr(L0_attn_W_out),
        "b_out": arr(L0_attn_b_out),
        "w_skip": arr(L0_attn_W_skip),
        "b_skip": arr(L0_attn_b_skip),
        "w_fc": arr(L0_ffn_w_fc).reshape(PHASES, HC, P, halves, HALF).transpose(0, 1, 3, 2, 4).reshape(UNITS, P, HALF),
        "w_proj": arr(L0_ffn_w_proj).reshape(KD, P, PHASES, HPP // HALF, HALF).transpose(2, 0, 3, 1, 4).reshape(UNITS, P, HALF),
    }
    arrays = {k: np.ascontiguousarray(v) for k, v in arrays.items()}
    nc = bacc.Bacc("TRN2", target_bir_lowering=False, num_devices=1)
    args = [nc.dram_tensor(k, v.shape, mybir.dt.uint32 if v.dtype.kind in "iu" else mybir.dt.from_np(v.dtype),
                           kind="ExternalInput").ap() for k, v in arrays.items()]
    out = nc.dram_tensor("out", (SEQS, TOK, D), F32, kind="ExternalOutput").ap()
    build(nc, *args, out)
    arrays["ids"] = arrays["ids"].view(np.uint32)
    got = run_bass_kernel_spmd(nc, [arrays], core_ids=[0])
    return got.results[0]["out"]
```

```python
from contextlib import ExitStack

import numpy as np

import concourse.bass as bass
from concourse import mybir

ALU = mybir.AluOpType
ACT = mybir.ActivationFunctionType
AX = mybir.AxisListType.X
F32 = mybir.dt.float32
BF16 = mybir.dt.bfloat16
U32 = mybir.dt.uint32

P = 128
SEQS, TOK, EMB = 16, 512, 64
D = TOK
S = 128
KT = TOK // P
KD = D // P
GATES = 3 * S
HID = 4 * D
PAIRS = SEQS // 2

PHASES = 4
HPP = HID // PHASES
HC = HPP // P
UNITS = PHASES * PAIRS
HALF = 256
UW = 2 * HALF
QB = 64
NB = UW // QB
UT = UW // P

QMAX = 15.0
MAGIC = 1.5 * 2.0 ** 23
SHRINKS = [float(np.float32(s)) for s in np.linspace(0.4, 1.0, 16)]
NS = len(SHRINKS)
EPS = 1e-5
ZR = 3
Z_BANK = (0, 1, 6)
SHRINK_SLOTS = ((0, 1), (2, 3), (4, 5), (6, 7, 8), (9, 10), (11, 12), (13, 14, 15), (16, 17))
RING = 3


def build(nc, ids, table, gamma, beta, w_in, b_in, w_out, b_out, w_skip, b_skip, w_fc, w_proj, out):
    ctx = ExitStack()
    with ctx:
        def sb(name, shape, dt=F32):
            return ctx.enter_context(nc.sbuf_tensor(name, shape, dt))

        def sem(name):
            return ctx.enter_context(nc.semaphore(name))

        xt_dram = nc.dram_tensor("xt_dram", [SEQS, P, 2 * KD * TOK], BF16).ap()
        acc_dram = nc.dram_tensor("acc_dram", [SEQS, P, KT * D], F32).ap()

        ident = sb("ident", [P, P])
        ones_mean = sb("ones_mean", [P, P])
        magic = sb("magic", [P, 1])
        neg_half = sb("neg_half", [P, 2 * KT])
        eps = sb("eps", [P, 2 * KT])
        neg_one = sb("neg_one", [P, KT])
        one = sb("one", [P, 1])
        idx_seen = sb("idx_seen", [P, 1])
        shrink_val = sb("shrink_val", [P, NS])
        shrink_rank = sb("shrink_rank", [P, NS])
        idx = sb("idx", [P, SEQS * KT], U32)
        wc = sb("wc", [P, KT, GATES + D])
        w_out_sb = sb("w_out_sb", [P, D])
        gamma_sb = sb("gamma_sb", [P, KD])
        beta_sb = sb("beta_sb", [P, KD])
        b_in_sb = sb("b_in_sb", [P, 3])
        c_in = sb("c_in", [P, 3])
        bias_bc = sb("bias_bc", [P, D])

        idx_now = sb("idx_now", [P, 2 * KT], U32)
        emb_next = sb("emb_next", [P, 2 * KT, EMB])
        emb2 = sb("emb2", [P, 2 * KT, 2, EMB])
        emb_c = sb("emb_c", [P, 2 * KT, EMB])
        lhs = sb("lhs", [P, 2, TOK])
        rhs = sb("rhs", [P, 2, D])
        gate_w = sb("gate_w", [P, 2, GATES])
        gate_x = sb("gate_x", [P, 2, TOK])
        cov = sb("cov", [EMB, 2, EMB])
        quad = sb("quad", [P, 2 * KT, EMB])
        scaled = sb("scaled", [P, 2 * KT, 2, EMB])
        var1 = sb("var1", [P, 2 * KT])
        stat = sb("stat", [P, 8, 2 * KT])
        mix = sb("mix", [P, 2, 4, TOK])
        gate_y = sb("gate_y", [P, 2, TOK])
        bn6 = sb("bn6", [P, 2 * KT, 6])
        mean_var = sb("mean_var", [P, 2 * KT, 2])
        stat3 = sb("stat3", [P, 2, 4, KT])
        res = sb("res", [P, 2, KT, D])
        xt = sb("xt", [P, 2, 2, KD, TOK], BF16)

        w_hi = sb("w_hi", [P, UNITS + 1, UW], BF16)
        w_lo = sb("w_lo", [P, UNITS + 1, UW], BF16)
        w_next = sb("w_next", [P, UW])
        w_raw = sb("w_raw", [P, UW])
        w_abs = sb("w_abs", [P, UW])
        w_norm = sb("w_norm", [P, UW])
        q_mag = sb("q_mag", [P, RING, UW])
        q_int = sb("q_int", [P, RING, UW], BF16)
        q_dif = sb("q_dif", [P, RING, UW])
        err = sb("err", [P, NS, NB])
        pick = sb("pick", [P, 2, NS, NB])
        qs = sb("qs", [P, 8, NB])
        w_scaled = sb("w_scaled", [P, UW])
        w_clip = sb("w_clip", [P, UW])
        w_q = sb("w_q", [P, UW])

        g_hi = sb("g_hi", [P, ZR, TOK], BF16)
        g_lo = sb("g_lo", [P, ZR, TOK], BF16)
        mlp_f32 = mix[:].rearrange("p e j t -> p (e j) t")
        relu_z = mlp_f32[:, 0:ZR, :]
        act_g = mlp_f32[:, ZR:2 * ZR, :]

        bank = [ctx.enter_context(nc.psum_tensor(f"bank{i}", [P, 512], F32)) for i in range(8)]
        Q_BANK = 7
        PROJ_BANK = ((4, 5), (0, 6))
        GATE_BANK = ((4, 5, 6), (0, 1, 3))
        H2_BANK = (4, 5, 6, 2, 0, 1, 3, 4)
        XT_BANK = (5, 6, 2, 1, 0, 3, 4, 5)

        consts_in = sem("consts_in")
        idx_in = sem("idx_in")
        pool_const = sem("pool_const")
        zero_gate = sem("zero_gate")
        bias_done = sem("bias_done")
        cin_ps = sem("cin_ps")
        wg_ready = sem("wg_ready")
        wmean_ps = sem("wmean_ps")
        wc_ready = sem("wc_ready")
        cin_ready = sem("cin_ready")
        emb_in = sem("emb_in")
        idx_ready = sem("idx_ready")
        emb2_ready = sem("emb2_ready")
        mean_ps = sem("mean_ps")
        et_ps = sem("et_ps")
        et_sb = sem("et_sb")
        emb_c_ready = sem("emb_c_ready")
        cov_ps = sem("cov_ps")
        cov_sb = sem("cov_sb")
        quad_ps = sem("quad_ps")
        proj_ps = sem("proj_ps")
        gate_w_ready = sem("gate_w_ready")
        skip_ready = sem("skip_ready")
        var1_ready = sem("var1_ready")
        r12_ready = sem("r12_ready")
        scaled_ready = sem("scaled_ready")
        scaled_ps = sem("scaled_ps")
        gate_x_ready = sem("gate_x_ready")
        gates_ps = sem("gates_ps")
        alpha_ready = sem("alpha_ready")
        tanh_ready = sem("tanh_ready")
        y_ready = sem("y_ready")
        h2_ps = sem("h2_ps")
        h2_sb = sem("h2_sb")
        mv_ready = sem("mv_ready")
        r3_ready = sem("r3_ready")
        x2_ready = sem("x2_ready")
        xt_ps = sem("xt_ps")
        xt_hi = sem("xt_hi")
        xt_lo = sem("xt_lo")
        stored = [sem("stored0"), sem("stored1")]
        stage_free = [sem("stage_free0"), sem("stage_free1")]
        w_in_sem = sem("w_landed")
        q_abs = sem("q_abs")
        q_norm = sem("q_norm")
        q_rounded = sem("q_rounded")
        q_int_ready = sem("q_int_ready")
        q_dif_ready = sem("q_dif_ready")
        q_sq_ready = sem("q_sq_ready")
        last_free = sem("last_free")
        w_kept = sem("w_kept")
        scale_ready = sem("scale_ready")
        w_scaled_ready = sem("w_scaled_ready")
        clip_ready = sem("clip_ready")
        w_q_ready = sem("w_q_ready")
        w_t_ps = sem("w_t_ps")
        w_hi_ready = sem("w_hi_ready")
        w_lo_ready = sem("w_lo_ready")
        dve_step = sem("dve_step")
        pool_step = sem("pool_step")
        dve_pro = sem("dve_pro")
        pool_pro = sem("pool_pro")
        x_in = [sem("x_in0"), sem("x_in1")]
        acc_in = [sem("acc_in0"), sem("acc_in1")]
        r3_part = sem("r3_part")
        quad_done = sem("quad_done")
        drive_done = sem("drive_done")
        scan_done = sem("scan_done")
        bn_done = sem("bn_done")
        acc_out = [sem("acc_out0"), sem("acc_out1")]
        z_ps = sem("z_ps")
        relu_ready = sem("relu_ready")
        g_ready = sem("g_ready")
        g_hi_ready = sem("g_hi_ready")
        g_lo_ready = sem("g_lo_ready")
        o_ps = sem("o_ps")
        o_added = sem("o_added")

        def blocks(ap):
            return ap.rearrange("p (b e) -> p b e", e=QB)

        def per_block(ap):
            return ap.unsqueeze(2).to_broadcast([P, NB, QB])

        def w_load(eng, u):
            eng.dma_start(w_next[:, 0:HALF], w_fc[bass.ds(u, 1), :, :].rearrange("a p n -> p (a n)")).then_inc(w_in_sem, 16)
            eng.dma_start(w_next[:, HALF:UW], w_proj[bass.ds(u, 1), :, :].rearrange("a p n -> p (a n)")).then_inc(w_in_sem, 16)

        def act_w_load(act, u):
            act.wait_ge(q_norm, u + 1)
            act.wait_ge(w_kept, u + 1)
            w_load(act, u + 1)

        def act_abs(act, u):
            act.wait_ge(w_in_sem, u * 32 + 32)
            act.activation(w_abs[:], w_next[:], ACT.Abs).then_inc(q_abs, 1)

        def act_round(act, u, s):
            if s == 0:
                act.wait_ge(q_norm, u + 1)
            if s >= RING:
                act.wait_ge(q_int_ready, u * (NS - 1) + s - RING + 1)
            act.activation(q_mag[:, s % RING, :], w_norm[:], ACT.Identity, bias=magic[:, 0:1],
                           scale=1.0 / SHRINKS[s]).then_inc(q_rounded, 1)

        def act_square(act, u, s):
            act.wait_ge(q_dif_ready, u * NS + s + 1)
            act.activation(q_dif[:, s % RING, :], q_dif[:, s % RING, :], ACT.Square).then_inc(q_sq_ready, 1)

        def act_shrink(act, u, s):
            if s < NS:
                act_round(act, u, s)
            if 2 <= s < NS + 2:
                act_square(act, u, s - 2)

        def slot(t, u):
            return t[:, bass.ds(u + 1, 1), :].rearrange("p a n -> p (a n)")

        def act_weights(act, m):
            act.wait_ge(w_t_ps, m + 1)
            act.activation(slot(w_hi, m - 1), bank[Q_BANK][:], ACT.Copy).then_inc(w_hi_ready, 1)

        def dve_link(dve, ins, base, n):
            ins.then_inc(dve_step, 1)
            dve.wait_ge(dve_step, base + n)

        QSTEPS = 13

        def dve_norm(dve, u):
            base = u * QSTEPS
            dve.wait_ge(w_in_sem, u * 32 + 32)
            dve_link(dve, dve.tensor_reduce(qs[:, 0, :], blocks(w_next[:]), AX, ALU.max, apply_absolute_value=True), base, 1)
            dve_link(dve, dve.tensor_scalar(qs[:, 1, :], qs[:, 0, :], 1e-8, 1.0 / QMAX, ALU.max, ALU.mult), base, 2)
            dve_link(dve, dve.reciprocal(qs[:, 2, :], qs[:, 1, :]), base, 3)
            dve.wait_ge(q_abs, u + 1)
            dve.tensor_tensor(blocks(w_norm[:]), blocks(w_abs[:]), per_block(qs[:, 2, :]), ALU.mult).then_inc(q_norm, 1)

        def dve_shrink(dve, u, s):
            if s < NS - 1:
                dve.wait_ge(q_rounded, u * NS + s + 1)
                dve.tensor_scalar(q_int[:, s % RING, :], q_mag[:, s % RING, :], MAGIC + QMAX, MAGIC, ALU.min,
                                  ALU.subtract).then_inc(q_int_ready, 1)
            if 1 <= s < NS + 1:
                r = s - 1
                if r < NS - 1:
                    dve.wait_ge(q_int_ready, u * (NS - 1) + r + 1)
                    dve.scalar_tensor_tensor(out=q_dif[:, r % RING, :], in0=q_int[:, r % RING, :], scalar=SHRINKS[r],
                                             in1=w_norm[:], op0=ALU.mult, op1=ALU.subtract).then_inc(q_dif_ready, 1)
                else:
                    dve.wait_ge(q_rounded, u * NS + r + 1)
                    dve.wait_ge(last_free, u + 1)
                    dve.scalar_tensor_tensor(out=q_dif[:, r % RING, :], in0=q_mag[:, r % RING, :], scalar=MAGIC,
                                             in1=w_norm[:], op0=ALU.subtract, op1=ALU.subtract).then_inc(q_dif_ready, 1)
            if 2 <= s < NS + 2:
                r = s - 2
                dve.wait_ge(q_sq_ready, u * NS + r + 1)
                ins = dve.tensor_reduce(err[:, r, :], blocks(q_dif[:, r % RING, :]), AX, ALU.add)
                if r == NS - 1:
                    ins.then_inc(dve_step, 1)
                if r == NS - 1 - RING:
                    ins.then_inc(last_free, 1)

        def dve_select(dve, u):
            base = u * QSTEPS
            by_block = err[:].rearrange("p s b -> p b s")
            dve.wait_ge(dve_step, base + 5)
            dve_link(dve, dve.tensor_reduce(qs[:, 3, :], by_block, AX, ALU.min), base, 6)
            least = qs[:, 3, :].unsqueeze(1).to_broadcast([P, NS, NB])
            rank = shrink_rank[:].unsqueeze(2).to_broadcast([P, NS, NB])
            value = shrink_val[:].unsqueeze(2).to_broadcast([P, NS, NB])
            dve_link(dve, dve.tensor_tensor(pick[:, 0, :, :], err[:], least, ALU.is_equal), base, 7)
            dve_link(dve, dve.tensor_tensor(pick[:, 1, :, :], pick[:, 0, :, :], rank, ALU.mult), base, 8)
            dve_link(dve, dve.tensor_reduce(qs[:, 4, :], pick[:, 1, :, :].rearrange("p s b -> p b s"), AX, ALU.max), base, 9)
            first = qs[:, 4, :].unsqueeze(1).to_broadcast([P, NS, NB])
            dve_link(dve, dve.tensor_tensor(pick[:, 0, :, :], pick[:, 1, :, :], first, ALU.is_equal), base, 10)
            dve_link(dve, dve.tensor_tensor(pick[:, 1, :, :], pick[:, 0, :, :], value, ALU.mult), base, 11)
            dve_link(dve, dve.tensor_reduce(qs[:, 5, :], pick[:, 1, :, :].rearrange("p s b -> p b s"), AX, ALU.max), base, 12)
            dve_link(dve, dve.tensor_tensor(qs[:, 6, :], qs[:, 5, :], qs[:, 1, :], ALU.mult), base, 13)
            dve.reciprocal(qs[:, 7, :], qs[:, 6, :]).then_inc(scale_ready, 1)

        def dve_clip(dve, m, n=4):
            dve.wait_ge(w_scaled_ready, m + 1)
            dve_link(dve, dve.tensor_scalar(w_clip[:], w_scaled[:], MAGIC, MAGIC + QMAX, ALU.add, ALU.min), m * QSTEPS, n)
            dve.tensor_scalar(w_scaled[:], w_clip[:], MAGIC - QMAX, MAGIC, ALU.max, ALU.subtract).then_inc(clip_ready, 1)

        def dve_weights(dve, m):
            dve.wait_ge(w_hi_ready, m + 1)
            dve.tensor_tensor(slot(w_lo, m - 1), bank[Q_BANK][:], slot(w_hi, m - 1), ALU.subtract).then_inc(w_lo_ready, 1)

        def pool_link(pool, ins, base, n):
            ins.then_inc(pool_step, 1)
            pool.wait_ge(pool_step, base + n)

        def pool_dequant(pool, m, base, n):
            pool.wait_ge(clip_ready, m + 1)
            pool_link(pool, pool.tensor_tensor(blocks(w_clip[:]), blocks(w_scaled[:]), per_block(qs[:, 6, :]), ALU.mult), base, n)
            pool_link(pool, pool.tensor_tensor(w_clip[:], w_clip[:], w_raw[:], ALU.subtract), base, n + 1)
            pool.tensor_tensor(w_q[:], w_raw[:], w_clip[:], ALU.add).then_inc(w_q_ready, 1)

        def pool_keep(pool, u):
            pool.wait_ge(w_q_ready, u + 1)
            pool.wait_ge(w_in_sem, u * 32 + 32)
            pool.tensor_tensor(w_raw[:], w_next[:], one[:].to_broadcast([P, UW]), ALU.mult).then_inc(w_kept, 1)

        def pool_scale(pool, u):
            pool.wait_ge(scale_ready, u + 1)
            pool.tensor_tensor(blocks(w_scaled[:]), blocks(w_raw[:]), per_block(qs[:, 7, :]), ALU.mult).then_inc(w_scaled_ready, 1)

        def pe_weights(pe, m):
            pe.wait_ge(w_q_ready, m + 1)
            for k in range(UT):
                last = pe.transpose(bank[Q_BANK][:, k * P:(k + 1) * P], w_q[:, k * P:(k + 1) * P], ident[:])
            last.then_inc(w_t_ps, 1)

        block = ctx.enter_context(nc.Block())

        @block.sync
        def _(sp):
            sp.dma_start(idx[:], ids).then_inc(idx_in, 16)
            w_load(sp, 0)
            w_in_v = w_in.rearrange("(k p) n -> p k n", p=P)
            w_skip_v = w_skip.rearrange("(k p) n -> p k n", p=P)
            sp.dma_start(wc[:, :, 0:GATES], w_in_v).then_inc(consts_in, 16)
            sp.dma_start(wc[:, :, GATES:GATES + D], w_skip_v).then_inc(consts_in, 16)
            sp.dma_start(gamma_sb[:], gamma).then_inc(consts_in, 16)
            sp.dma_start(beta_sb[:], beta).then_inc(consts_in, 16)
            sp.dma_start(b_in_sb[:], b_in).then_inc(consts_in, 16)
            sp.dma_start(w_out_sb[:], w_out).then_inc(consts_in, 16)
            sp.dma_start(bias_bc[:], b_out.partition_broadcast(P)).then_inc(consts_in, 16)
            sp.dma_start(quad[:].rearrange("p a b -> p (a b)"), b_skip.partition_broadcast(P)).then_inc(consts_in, 16)

            with sp.Fori(0, PAIRS) as i:
                for e in range(2):
                    sp.wait_ge(xt_hi, i * 2 * KD + (e + 1) * KD)
                    sp.wait_ge(xt_lo, i * 2 * KD + (e + 1) * KD)
                    sp.dma_start(xt_dram[bass.ds(i * 2 + e, 1), :, :].rearrange("a p n -> p (a n)"),
                                 xt[:, e].rearrange("p a k t -> p (a k t)")).then_inc(stored[e], 16)
                    sp.dma_start(acc_dram[bass.ds(i * 2 + e, 1), :, :].rearrange("a p n -> p (a n)"),
                                 res[:, e].rearrange("p k d -> p (k d)")).then_inc(stored[e], 16)
                for e in range(2):
                    sp.wait_ge(stored[e], i * 32 + 32)
                    sp.nop().then_inc(stage_free[e], 1)

            def load_x(g, e):
                sp.dma_start(xt[:, e].rearrange("p a k t -> p (a k t)"),
                             xt_dram[bass.ds(g, 1), :, :].rearrange("a p n -> p (a n)")).then_inc(x_in[e], 16)

            def load_acc(g, e):
                sp.dma_start(res[:, e].rearrange("p k d -> p (k d)"),
                             acc_dram[bass.ds(g, 1), :, :].rearrange("a p n -> p (a n)")).then_inc(acc_in[e], 16)

            def after_group(n, g, g_next, e, to_out):
                if g_next is not None:
                    sp.wait_ge(z_ps, n * 2 * HC + (e + 1) * HC)
                    load_x(g_next, e)
                sp.wait_ge(o_added, n * 2 * KT + KT * (e + 1) + KT)
                if to_out:
                    sp.dma_start(out[bass.ds(g, 1), :, :].rearrange("a (k p) d -> p (a k) d", p=P),
                                 res[:, e]).then_inc(acc_out[e], 16)
                else:
                    sp.dma_start(acc_dram[bass.ds(g, 1), :, :].rearrange("a p n -> p (a n)"),
                                 res[:, e].rearrange("p k d -> p (k d)")).then_inc(acc_out[e], 16)
                sp.wait_ge(acc_out[e], n * 16 + 16)
                if g_next is not None:
                    load_acc(g_next, e)

            for e in range(2):
                load_x(e, e)
                load_acc(e, e)
            for ph in range(PHASES):
                last_phase = ph == PHASES - 1
                with sp.Fori(0, PAIRS - 1) as i:
                    for e in range(2):
                        after_group(i + ph * PAIRS, i * 2 + e, i * 2 + 2 + e, e, last_phase)
                for e in range(2):
                    after_group(ph * PAIRS + PAIRS - 1, SEQS - 2 + e, e if ph < PHASES - 1 else None, e, last_phase)

        @block.gpsimd
        def _(pool):
            pool.memset(ident[:], 0.0).then_inc(pool_pro, 1)
            pool.wait_ge(pool_pro, 1)
            pool.affine_select(out=ident[:], in_=ident[:], compare_op=ALU.not_equal, fill=1.0, base=0,
                               pattern=[[-1, P]], channel_multiplier=1).then_inc(pool_const, 1)
            pool.memset(ones_mean[:], 1.0 / TOK).then_inc(pool_const, 1)
            pool.memset(magic[:], MAGIC).then_inc(pool_const, 1)
            for s in range(NS):
                pool.memset(shrink_val[:, s:s + 1], SHRINKS[s])
                pool.memset(shrink_rank[:, s:s + 1], float(NS - s)).then_inc(pool_const, 1)
            for t in (w_raw, w_q):
                pool.memset(t[:], 0.0)
            pool.memset(w_scaled[:], 0.0).then_inc(w_scaled_ready, 1)
            pool.memset(eps[:], EPS)
            pool.memset(neg_one[:], -1.0)
            pool.memset(one[:], 1.0)
            pool.memset(neg_half[:], -0.5).then_inc(pool_pro, 1)
            pool.wait_ge(pool_pro, 2)

            def gather(i):
                pool.tensor_copy(idx_now[:], idx[:, bass.ds(i * 2 * KT, 2 * KT)]).then_inc(idx_ready, 1)
                pool.wait_ge(idx_ready, i + 1)
                pool.tensor_tensor(idx_seen[:], neg_one[:, 0:1], neg_one[:, 0:1], ALU.mult)
                for k in range(2 * KT):
                    pool.indirect_dma_start(emb_next[:, k, :], None, table,
                                            bass.IndirectOffsetOnAxis(ap=idx_now[:, k:k + 1], axis=0)).then_inc(emb_in, 16)

            POOL_STEPS = 6 + 2 * 2 + 2
            TAIL_STEPS = 2

            def rsqrt_pair(i):
                base = i * POOL_STEPS + 2
                pool.wait_ge(var1_ready, i + 1)
                pool_link(pool, pool.tensor_tensor(stat[:, 0, :], var1[:], eps[:], ALU.add), base, 1)
                pool_link(pool, pool.tensor_tensor(stat[:, 1, :], stat[:, 0, :], neg_half[:], ALU.pow), base, 2)
                pool_link(pool, pool.tensor_tensor(stat[:, 2, :], var1[:], stat[:, 1, :], ALU.mult), base, 3)
                pool_link(pool, pool.tensor_tensor(stat[:, 3, :], stat[:, 2, :], stat[:, 1, :], ALU.mult), base, 4)
                pool_link(pool, pool.tensor_tensor(stat[:, 4, :], stat[:, 3, :], eps[:], ALU.add), base, 5)
                pool_link(pool, pool.tensor_tensor(stat[:, 5, :], stat[:, 4, :], neg_half[:], ALU.pow), base, 6)
                pool.tensor_tensor(stat[:, 6, :], stat[:, 5, :], stat[:, 1, :], ALU.mult).then_inc(r12_ready, 1)

            def rsqrt_mlp(i, e):
                base = i * POOL_STEPS + 8 + 2 * e
                pool.wait_ge(mv_ready, i * 2 + e + 1)
                mv = mean_var[:, e * KT:(e + 1) * KT, :]
                pool_link(pool, pool.tensor_tensor(stat3[:, e, 0, :], mv[:, :, 1], eps[:, 0:KT], ALU.add), base, 1)
                pool_link(pool, pool.tensor_tensor(stat3[:, e, 1, :], stat3[:, e, 0, :], neg_half[:, 0:KT], ALU.pow), base, 2)
                pool.tensor_tensor(stat3[:, e, 2, :], mv[:, :, 0], neg_one[:], ALU.mult).then_inc(r3_part, 1)
                pool.wait_ge(r3_part, i * 2 + e + 1)
                pool.tensor_tensor(stat3[:, e, 3, :], stat3[:, e, 2, :], stat3[:, e, 1, :], ALU.mult).then_inc(r3_ready, 1)

            pool.wait_ge(idx_in, 16)
            gather(0)

            def mixer_step(i, more):
                if more:
                    pool.wait_ge(emb2_ready, i + 1)
                    pool.wait_ge(emb_in, i * 2 * KT * 16 + 2 * KT * 16)
                    gather(i + 1)
                pool_dequant(pool, i, i * POOL_STEPS, 1)
                pool_keep(pool, i)
                rsqrt_pair(i)
                rsqrt_mlp(i, 0)
                rsqrt_mlp(i, 1)
                pool_scale(pool, i)

            with pool.Fori(0, PAIRS - 1) as i:
                mixer_step(i, True)
            mixer_step(PAIRS - 1, False)

            def low_part(n, k):
                pool.wait_ge(g_hi_ready, n * 2 * HC + k + 1)
                pool.tensor_tensor(g_lo[:, k % ZR, :], act_g[:, k % ZR, :], g_hi[:, k % ZR, :], ALU.subtract).then_inc(g_lo_ready, 1)

            def mlp_step(n, finish, quant):
                m = n + PAIRS
                if finish:
                    pool_dequant(pool, m, n * TAIL_STEPS + PAIRS * POOL_STEPS, 1)
                low_part(n, 0)
                if quant:
                    pool_keep(pool, m)
                for k in range(1, 2 * HC):
                    low_part(n, k)
                if quant:
                    pool_scale(pool, m)

            for ph in range(PHASES - 1):
                with pool.Fori(0, PAIRS) as i:
                    mlp_step(i + ph * PAIRS, True, True)
            mlp_step((PHASES - 1) * PAIRS, True, False)
            with pool.Fori(1, PAIRS) as i:
                mlp_step(i + (PHASES - 1) * PAIRS, False, False)

        @block.tensor
        def _(pe):
            pe.wait_ge(consts_in, 8 * 16)
            pe.wait_ge(pool_const, 3 + NS)
            for j in range(3):
                for k in range(KD):
                    last = pe.matmul(bank[0][:, j:j + 1], wc[:, k, j * S:(j + 1) * S], beta_sb[:, k:k + 1],
                                     start=(k == 0), stop=(k == KD - 1))
            last.then_inc(cin_ps, 1)
            pe.wait_ge(wg_ready, 1)
            for k in range(KD):
                pe.matmul(bank[1][:, 0:GATES], ones_mean[:], wc[:, k, 0:GATES], start=(k == 0), stop=(k == KD - 1))
            for k in range(KD):
                last = pe.matmul(bank[2][:], ones_mean[:], wc[:, k, GATES:GATES + D], start=(k == 0), stop=(k == KD - 1))
            last.then_inc(wmean_ps, 1)
            pe.wait_ge(wc_ready, 1)
            pe.wait_ge(zero_gate, 1)

            def emb_of(e, k):
                return emb2[:, e * KT + k, 0, :]

            with pe.Fori(0, PAIRS) as i:
                pe.wait_ge(emb2_ready, i + 1)
                for e in range(2):
                    for k in range(KT):
                        last = pe.matmul(bank[0][:, e * EMB:(e + 1) * EMB], ones_mean[:], emb_of(e, k),
                                         start=(k == 0), stop=(k == KT - 1))
                last.then_inc(mean_ps, 1)
                for e in range(2):
                    for k in range(KT):
                        last = pe.transpose(bank[2 + e][0:EMB, k * P:(k + 1) * P], emb_of(e, k), ident[:])
                    last.then_inc(et_ps, 1)

                def project(e):
                    ba, bb = PROJ_BANK[e]
                    for k in range(KT):
                        both = emb2[:, e * KT + k, :, :].rearrange("p a b -> p (a b)")
                        pe.matmul(bank[ba][:, 0:GATES], both, wc[:, k, 0:GATES], start=(k == 0), stop=(k == KT - 1))
                        last = pe.matmul(bank[bb][:], both, wc[:, k, GATES:GATES + D], start=(k == 0), stop=(k == KT - 1))
                    last.then_inc(proj_ps, 1)

                project(0)
                pe_weights(pe, i)
                pe.wait_ge(emb_c_ready, i + 1)
                for e in range(2):
                    for k in range(KT):
                        last = pe.matmul(bank[0][0:EMB, P + e * EMB:P + (e + 1) * EMB], emb_c[:, e * KT + k, :],
                                         emb_c[:, e * KT + k, :], start=(k == 0), stop=(k == KT - 1))
                last.then_inc(cov_ps, 1)
                pe.wait_ge(et_sb, 2 * i + 2)
                pe.wait_ge(cov_sb, i + 1)
                for e in range(2):
                    for k in range(KT):
                        m = e * KT + k
                        last = pe.matmul(bank[1][:, m * EMB:(m + 1) * EMB], lhs[0:EMB, e, k * P:(k + 1) * P],
                                         cov[:, e, :], start=True, stop=True)
                last.then_inc(quad_ps, 1)
                project(1)
                pe.wait_ge(scaled_ready, i + 1)
                for e in range(2):
                    for k in range(KT):
                        last = pe.transpose(bank[2 + e][:, k * P:(k + 1) * P],
                                            scaled[:, e * KT + k, :, :].rearrange("p a b -> p (a b)"), ident[:])
                    last.then_inc(scaled_ps, 1)
                for e in range(2):
                    pe.wait_ge(gate_x_ready, 2 * i + e + 1)
                    pe.wait_ge(gate_w_ready, 2 * i + 2)
                    pe.wait_ge(skip_ready, 2 * i + 2)
                    if e == 1:
                        pe.wait_ge(gate_x_ready, 2 * i + 2)
                    for j in range(3):
                        b = GATE_BANK[e][j]
                        pe.matmul(bank[b][:], gate_w[:, e, j * S:(j + 1) * S], gate_x[:, e, :],
                                  start=True, stop=True).then_inc(gates_ps, 1)
                for e in range(2):
                    pe.wait_ge(y_ready, 2 * i + e + 1)
                    for k in range(KT):
                        m = e * KT + k
                        if m == 7:
                            pe.wait_ge(h2_sb, 2 * KT * i + 1)
                        pe.matmul(bank[H2_BANK[m]][:], lhs[:, e, k * P:(k + 1) * P], rhs[:, e, :], start=True, stop=False)
                        pe.matmul(bank[H2_BANK[m]][:], gate_y[:, e, k * P:(k + 1) * P], w_out_sb[:],
                                  start=False, stop=True).then_inc(h2_ps, 1)
                for e in range(2):
                    pe.wait_ge(x2_ready, 2 * i + e + 1)
                    pe.wait_ge(h2_sb, 2 * KT * i + (6, 8)[e])
                    for d in range(KD):
                        m = e * KD + d
                        if m == 7:
                            pe.wait_ge(xt_lo, 2 * KD * i + 1)
                        for k in range(KT):
                            last = pe.transpose(bank[XT_BANK[m]][:, k * P:(k + 1) * P], mix[:, e, k, d * P:(d + 1) * P], ident[:])
                        last.then_inc(xt_ps, 1)

            def up(n, unit0, e, c):
                if c == 0:
                    pe.wait_ge(x_in[e], n * 16 + 16)
                z = bank[Z_BANK[(e * HC + c) % ZR]][:]
                for d in range(KD):
                    at, t = unit0 + 1 + 2 * c + d // 2, d % 2
                    hi, lo = w_hi[:, at, t * P:(t + 1) * P], w_lo[:, at, t * P:(t + 1) * P]
                    pe.matmul(z, hi, xt[:, e, 0, d, :], start=(d == 0), stop=False)
                    pe.matmul(z, hi, xt[:, e, 1, d, :], start=False, stop=False)
                    last = pe.matmul(z, lo, xt[:, e, 0, d, :], start=False, stop=(d == KD - 1))
                last.then_inc(z_ps, 1)

            def down(n, unit0, e, c):
                j, at = e * HC + c, unit0 + 1 + 2 * c
                w_h, w_l = w_hi[:, at:at + 2, HALF:UW], w_lo[:, at:at + 2, HALF:UW]
                pe.wait_ge(g_hi_ready, n * 2 * HC + j + 1)
                for k in range(KT):
                    o = bank[2 + k][:].rearrange("p (a b) -> p a b", b=HALF)
                    if c == 0:
                        pe.wait_ge(o_added, n * 2 * KT + e * KT + k + 1)
                    ghi = g_hi[:, j % ZR, k * P:(k + 1) * P]
                    pe.matmul(o, ghi, w_h, start=(c == 0), stop=False)
                    pe.matmul(o, ghi, w_l, start=False, stop=False)
                pe.wait_ge(g_lo_ready, n * 2 * HC + j + 1)
                for k in range(KT):
                    o = bank[2 + k][:].rearrange("p (a b) -> p a b", b=HALF)
                    last = pe.matmul(o, g_lo[:, j % ZR, k * P:(k + 1) * P], w_h, start=False, stop=(c == HC - 1))
                    if c == HC - 1:
                        last.then_inc(o_ps, 1)

            def mlp_step(ph, n, finish):
                slices = [(e, c) for e in range(2) for c in range(HC)]
                for j, (e, c) in enumerate(slices):
                    if j == ZR and finish:
                        pe.wait_ge(w_lo_ready, n + PAIRS + 1)
                    up(n, ph * PAIRS, e, c)
                    if j == ZR - 1 and finish:
                        pe_weights(pe, n + PAIRS)
                    if j >= ZR - 1:
                        down(n, ph * PAIRS, *slices[j - ZR + 1])
                for j in range(len(slices) - ZR + 1, len(slices)):
                    down(n, ph * PAIRS, *slices[j])

            for ph in range(PHASES):
                pe.wait_ge(w_lo_ready, (ph + 1) * PAIRS)
                if ph < PHASES - 1:
                    with pe.Fori(0, PAIRS) as i:
                        mlp_step(ph, i + ph * PAIRS, True)
                else:
                    mlp_step(ph, ph * PAIRS, True)
                    with pe.Fori(1, PAIRS) as i:
                        mlp_step(ph, i + ph * PAIRS, False)

        @block.scalar
        def _(act):
            for e in range(2):
                act.nop().then_inc(stage_free[e], 1)
            act.wait_ge(pool_const, 3 + NS)
            act.wait_ge(cin_ready, 1)
            with act.Fori(0, PAIRS) as i:
                act_abs(act, i)
                for e in range(2):
                    act.wait_ge(et_ps, 2 * i + e + 1)
                    act.activation(lhs[0:EMB, e, :], bank[2 + e][0:EMB, :], ACT.Copy)
                    act.activation(rhs[0:EMB, e, :], bank[2 + e][0:EMB, :], ACT.Copy, scale=0.125).then_inc(et_sb, 1)
                act_shrink(act, i, 0)
                act_shrink(act, i, 1)
                act.wait_ge(cov_ps, i + 1)
                act.activation(cov[:].rearrange("p a b -> p (a b)"), bank[0][0:EMB, P:2 * P], ACT.Copy,
                               scale=1.0 / (EMB * D)).then_inc(cov_sb, 1)
                act_shrink(act, i, 2)
                act_weights(act, i)
                act_w_load(act, i)
                act_shrink(act, i, 3)
                for e in range(2):
                    act.wait_ge(proj_ps, 2 * i + e + 1)
                    ba, bb = PROJ_BANK[e]
                    act.activation(gate_w[0:EMB, e, :], bank[ba][0:EMB, 0:GATES], ACT.Copy, scale=0.125).then_inc(gate_w_ready, 1)
                    act.activation(rhs[EMB:P, e, :], bank[bb][EMB:P, :], ACT.Copy, scale=0.125).then_inc(skip_ready, 1)
                    act_shrink(act, i, 4 + e)
                act_shrink(act, i, 6)
                act_shrink(act, i, 7)
                for e in range(2):
                    act.wait_ge(scaled_ps, 2 * i + e + 1)
                    act.activation(gate_x[:, e, :], bank[2 + e][:], ACT.Copy)
                    act.activation(lhs[EMB:P, e, :], bank[2 + e][EMB:P, :], ACT.Copy).then_inc(gate_x_ready, 1)
                act_shrink(act, i, 8)
                for e in range(2):
                    b0, _, b2 = GATE_BANK[e]
                    act.wait_ge(gates_ps, 6 * i + 3 * e + 3)
                    act.activation(mix[:, e, 0, :], bank[b0][:], ACT.Sigmoid, bias=c_in[:, 0:1]).then_inc(alpha_ready, 1)
                    act.activation(gate_y[:, e, :], bank[b2][:], ACT.Tanh, bias=c_in[:, 2:3]).then_inc(tanh_ready, 1)
                    act_shrink(act, i, 9 + e)
                act_shrink(act, i, 11)
                act_shrink(act, i, 12)
                act_shrink(act, i, 13)
                for e in range(2):
                    act.wait_ge(r3_ready, 2 * i + e + 1)
                    for k in range(KT):
                        last = act.activation(mix[:, e, k, :], res[:, e, k, :], ACT.Identity, bias=stat3[:, e, 3, k:k + 1],
                                              scale=stat3[:, e, 1, k:k + 1])
                    last.then_inc(x2_ready, 1)
                    act_shrink(act, i, 14 + e)
                for e in range(2):
                    act.wait_ge(stage_free[e], i + 1)
                    for d in range(KD):
                        m = e * KD + d
                        act.wait_ge(xt_ps, 2 * KD * i + m + 1)
                        act.activation(xt[:, e, 0, d, :], bank[XT_BANK[m]][:], ACT.Copy).then_inc(xt_hi, 1)
                    act_shrink(act, i, 16 + e)

            def mlp_step(n, finish, quant, load):
                m = n + PAIRS
                if quant:
                    act_abs(act, m)
                for k in range(2 * HC):
                    act.wait_ge(z_ps, n * 2 * HC + k + 1)
                    act.activation(relu_z[:, k % ZR, :], bank[Z_BANK[k % ZR]][:], ACT.Relu).then_inc(relu_ready, 1)
                    act.wait_ge(relu_ready, n * 2 * HC + k + 1)
                    act.activation(act_g[:, k % ZR, :], relu_z[:, k % ZR, :], ACT.Square).then_inc(g_ready, 1)
                    if quant:
                        for s in SHRINK_SLOTS[k]:
                            act_shrink(act, m, s)
                    if k == 1 and finish:
                        act_weights(act, m)
                    if k == 3 and load:
                        act_w_load(act, m)

            for ph in range(PHASES - 1):
                if ph < PHASES - 2:
                    with act.Fori(0, PAIRS) as i:
                        mlp_step(i + ph * PAIRS, True, True, True)
                else:
                    with act.Fori(0, PAIRS - 1) as i:
                        mlp_step(i + ph * PAIRS, True, True, True)
                    mlp_step(ph * PAIRS + PAIRS - 1, True, True, False)
            mlp_step((PHASES - 1) * PAIRS, True, False, False)
            with act.Fori(1, PAIRS) as i:
                mlp_step(i + (PHASES - 1) * PAIRS, False, False, False)

        @block.vector
        def _(dve):
            dve.memset(qs[:], 0.0)
            dve.memset(gate_w[EMB:P, :, :], 0.0).then_inc(zero_gate, 1)
            dve.wait_ge(zero_gate, 1)
            dve.wait_ge(consts_in, 8 * 16)
            dve.tensor_tensor(bias_bc[:], bias_bc[:], quad[:].rearrange("p a b -> p (a b)"), ALU.add).then_inc(bias_done, 1)
            dve.wait_ge(cin_ps, 1)
            dve.tensor_tensor(c_in[:], bank[0][:, 0:3], b_in_sb[:], ALU.add).then_inc(cin_ready, 1)
            for k in range(KD):
                last = dve.tensor_scalar(wc[:, k, 0:GATES], wc[:, k, 0:GATES], gamma_sb[:, k:k + 1], None, ALU.mult)
            last.then_inc(wg_ready, 1)
            dve.wait_ge(wg_ready, 1)
            dve.wait_ge(wmean_ps, 1)
            for k in range(KD):
                dve.tensor_tensor(wc[:, k, 0:GATES], wc[:, k, 0:GATES], bank[1][:, 0:GATES], ALU.subtract)
                last = dve.tensor_tensor(wc[:, k, GATES:GATES + D], wc[:, k, GATES:GATES + D], bank[2][:], ALU.subtract)
            last.then_inc(wc_ready, 1)
            dve.wait_ge(bias_done, 1)
            dve.wait_ge(pool_const, 3 + NS)
            dve.memset(bn6[:, 0, 0:1], 0.0).then_inc(o_added, KT)

            with dve.Fori(0, PAIRS) as i:
                dve.wait_ge(emb_in, i * 2 * KT * 16 + 2 * KT * 16)
                dve.tensor_copy(emb2[:], emb_next[:].unsqueeze(2).to_broadcast([P, 2 * KT, 2, EMB])).then_inc(emb2_ready, 1)
                dve_norm(dve, i)
                dve_clip(dve, i)
                dve.wait_ge(emb2_ready, i + 1)
                dve.wait_ge(mean_ps, i + 1)
                for e in range(2):
                    mean = bank[0][:, e * EMB:(e + 1) * EMB].unsqueeze(1).to_broadcast([P, KT, EMB])
                    last = dve.tensor_tensor(emb_c[:, e * KT:(e + 1) * KT, :], emb2[:, e * KT:(e + 1) * KT, 0, :], mean, ALU.subtract)
                last.then_inc(emb_c_ready, 1)
                for s in range(0, 4):
                    dve_shrink(dve, i, s)
                dve_weights(dve, i)
                dve.wait_ge(quad_ps, i + 1)
                dve.tensor_tensor(quad[:], bank[1][:].rearrange("p (a b) -> p a b", b=EMB), emb2[:, :, 0, :],
                                  ALU.mult).then_inc(quad_done, 1)
                dve.wait_ge(quad_done, i + 1)
                dve.tensor_reduce(var1[:], quad[:], AX, ALU.add).then_inc(var1_ready, 1)
                for s in range(4, 8):
                    dve_shrink(dve, i, s)
                dve.wait_ge(r12_ready, i + 1)
                dve.tensor_tensor(scaled[:, :, 0, :], emb2[:, :, 0, :], stat[:, 6, :].unsqueeze(2).to_broadcast([P, 2 * KT, EMB]), ALU.mult)
                dve.tensor_tensor(scaled[:, :, 1, :], emb2[:, :, 0, :], stat[:, 1, :].unsqueeze(2).to_broadcast([P, 2 * KT, EMB]),
                                  ALU.mult).then_inc(scaled_ready, 1)
                dve_shrink(dve, i, 8)
                for e in range(2):
                    b1 = GATE_BANK[e][1]
                    alpha, keep, drive, state = (mix[:, e, j, :] for j in range(4))
                    dve.wait_ge(alpha_ready, 2 * i + e + 1)
                    dve.tensor_scalar(keep, alpha, -1.0, 1.0, ALU.mult, ALU.add)
                    dve.scalar_tensor_tensor(out=drive, in0=bank[b1][:], scalar=c_in[:, 1:2], in1=alpha, op0=ALU.add,
                                             op1=ALU.mult).then_inc(drive_done, 1)
                    dve_shrink(dve, i, 9 + e)
                    dve.wait_ge(drive_done, 2 * i + e + 1)
                    dve.tensor_tensor_scan(state, keep, drive, 0.0, ALU.mult, ALU.add).then_inc(scan_done, 1)
                    dve.wait_ge(scan_done, 2 * i + e + 1)
                    dve.wait_ge(tanh_ready, 2 * i + e + 1)
                    dve.tensor_tensor(gate_y[:, e, :], state, gate_y[:, e, :], ALU.mult).then_inc(y_ready, 1)
                dve_shrink(dve, i, 11)
                for e in range(2):
                    dve.wait_ge(stage_free[e], i + 1)
                    for k in range(KT):
                        m = e * KT + k
                        dve.wait_ge(h2_ps, 2 * KT * i + m + 1)
                        dve.tensor_tensor(res[:, e, k, :], bank[H2_BANK[m]][:], bias_bc[:], ALU.add).then_inc(h2_sb, 1)
                        if k >= 1:
                            dve.wait_ge(h2_sb, 2 * KT * i + m)
                            dve.bn_stats(bn6[:, m - 1, :], res[:, e, k - 1, :])
                    dve.wait_ge(h2_sb, 2 * KT * i + (e + 1) * KT)
                    dve.bn_stats(bn6[:, e * KT + KT - 1, :], res[:, e, KT - 1, :]).then_inc(bn_done, 1)
                    dve.wait_ge(bn_done, 2 * i + e + 1)
                    dve_shrink(dve, i, 12 + e)
                    for k in range(KT):
                        last = dve.bn_aggr(mean_var[:, e * KT + k, :], bn6[:, e * KT + k, :])
                    last.then_inc(mv_ready, 1)
                dve_shrink(dve, i, 14)
                dve_shrink(dve, i, 15)
                for e in range(2):
                    for d in range(KD):
                        m = e * KD + d
                        dve.wait_ge(xt_hi, 2 * KD * i + m + 1)
                        dve.tensor_tensor(xt[:, e, 1, d, :], bank[XT_BANK[m]][:], xt[:, e, 0, d, :],
                                          ALU.subtract).then_inc(xt_lo, 1)
                    dve_shrink(dve, i, 16 + e)
                dve_select(dve, i)

            def add_group(n, e):
                dve.wait_ge(acc_in[e], n * 16 + 16)
                for k in range(KT):
                    dve.wait_ge(o_ps, n * 2 * KT + e * KT + k + 1)
                    dve.tensor_tensor(res[:, e, k, :], bank[2 + k][:], res[:, e, k, :], ALU.add).then_inc(o_added, 1)

            def mlp_step(n, finish, quant):
                m = n + PAIRS
                if quant:
                    dve_norm(dve, m)
                if finish:
                    dve_clip(dve, m, 4 if quant else 1)
                for k in range(2 * HC):
                    if k == HC + 1:
                        add_group(n, 0)
                    dve.wait_ge(g_ready, n * 2 * HC + k + 1)
                    dve.tensor_scalar(g_hi[:, k % ZR, :], act_g[:, k % ZR, :], 1.0, None, ALU.mult).then_inc(g_hi_ready, 1)
                    if quant:
                        for s in SHRINK_SLOTS[k]:
                            dve_shrink(dve, m, s)
                    if k == 1 and finish:
                        dve_weights(dve, m)
                if quant:
                    dve_select(dve, m)
                add_group(n, 1)

            for ph in range(PHASES - 1):
                with dve.Fori(0, PAIRS) as i:
                    mlp_step(i + ph * PAIRS, True, True)
            mlp_step((PHASES - 1) * PAIRS, True, False)
            with dve.Fori(1, PAIRS) as i:
                mlp_step(i + (PHASES - 1) * PAIRS, False, False)


def kernel(x, L0_tok_weight, L0_attn_gamma, L0_attn_beta, L0_attn_W_in, L0_attn_b_in, L0_attn_W_out, L0_attn_b_out,
           L0_attn_W_skip, L0_attn_b_skip, L0_ffn_w_fc, L0_ffn_w_proj):
    import concourse.bacc as bacc
    from concourse.bass_utils import run_bass_kernel_spmd

    arr = np.asarray
    halves = D // HALF
    arrays = {
        "ids": arr(x).reshape(SEQS * KT, P).T,
        "table": arr(L0_tok_weight),
        "gamma": arr(L0_attn_gamma).reshape(KD, P).T,
        "beta": arr(L0_attn_beta).reshape(KD, P).T,
        "w_in": arr(L0_attn_W_in),
        "b_in": arr(L0_attn_b_in).reshape(3, S).T,
        "w_out": arr(L0_attn_W_out),
        "b_out": arr(L0_attn_b_out),
        "w_skip": arr(L0_attn_W_skip),
        "b_skip": arr(L0_attn_b_skip),
        "w_fc": arr(L0_ffn_w_fc).reshape(PHASES, HC, P, halves, HALF).transpose(0, 1, 3, 2, 4).reshape(UNITS, P, HALF),
        "w_proj": arr(L0_ffn_w_proj).reshape(halves, KD // halves, P, PHASES, HC, P).transpose(3, 4, 0, 2, 1, 5)
        .reshape(UNITS, P, HALF),
    }
    arrays = {k: np.ascontiguousarray(v) for k, v in arrays.items()}
    nc = bacc.Bacc("TRN2", target_bir_lowering=False, num_devices=1)
    args = [nc.dram_tensor(k, v.shape, mybir.dt.uint32 if v.dtype.kind in "iu" else mybir.dt.from_np(v.dtype),
                           kind="ExternalInput").ap() for k, v in arrays.items()]
    out = nc.dram_tensor("out", (SEQS, TOK, D), F32, kind="ExternalOutput").ap()
    build(nc, *args, out)
    arrays["ids"] = arrays["ids"].view(np.uint32)
    got = run_bass_kernel_spmd(nc, [arrays], core_ids=[0])
    return got.results[0]["out"]
```

```python
from contextlib import ExitStack

import numpy as np

import concourse.bass as bass
from concourse import mybir

ALU = mybir.AluOpType
ACT = mybir.ActivationFunctionType
AX = mybir.AxisListType.X
F32 = mybir.dt.float32
BF16 = mybir.dt.bfloat16
U32 = mybir.dt.uint32

P = 128
SEQS, TOK, EMB = 16, 512, 64
D = TOK
S = 128
KT = TOK // P
KD = D // P
GATES = 3 * S
HID = 4 * D
PAIRS = SEQS // 2

PHASES = 4
HPP = HID // PHASES
HC = HPP // P
UNITS = PHASES * PAIRS
HALF = 256
UW = 2 * HALF
QB = 64
NB = UW // QB
UT = UW // P

QMAX = 15.0
MAGIC = 1.5 * 2.0 ** 23
SHRINKS = [float(np.float32(s)) for s in np.linspace(0.4, 1.0, 16)]
NS = len(SHRINKS)
EPS = 1e-5
ZR = 3
Z_BANK = (0, 1, 6)
SLOTS = NS + 3
SHRINK_SLOTS = ((0, 1), (2, 3), (4, 5), (6, 7, 8), (9, 10), (11, 12, 13), (14, 15), (16, 17, 18))
RING = 3


def build(nc, ids, table, gamma, beta, w_in, b_in, w_out, b_out, w_skip, b_skip, w_fc, w_proj, out):
    ctx = ExitStack()
    with ctx:
        def sb(name, shape, dt=F32):
            return ctx.enter_context(nc.sbuf_tensor(name, shape, dt))

        def sem(name):
            return ctx.enter_context(nc.semaphore(name))

        xt_dram = nc.dram_tensor("xt_dram", [SEQS, P, 2 * KD * TOK], BF16).ap()
        acc_dram = nc.dram_tensor("acc_dram", [SEQS, P, KT * D], F32).ap()

        ident = sb("ident", [P, P])
        ones_mean = sb("ones_mean", [P, P])
        magic = sb("magic", [P, 1])
        neg_half = sb("neg_half", [P, KT, 2])
        eps = sb("eps", [P, KT, 2])
        neg_one = sb("neg_one", [P, KT])
        one = sb("one", [P, 1])
        idx_seen = sb("idx_seen", [P, 1])
        shrink_val = sb("shrink_val", [P, NS])
        shrink_rank = sb("shrink_rank", [P, NS])
        idx = sb("idx", [P, SEQS * KT], U32)
        wc = sb("wc", [P, KT, GATES + D])
        w_out_sb = sb("w_out_sb", [P, D])
        gamma_sb = sb("gamma_sb", [P, KD])
        beta_sb = sb("beta_sb", [P, KD])
        b_in_sb = sb("b_in_sb", [P, 3])
        c_in = sb("c_in", [P, 3])
        ones_bf = sb("ones_bf", [P, P], BF16)
        bias3 = sb("bias3", [P, D], BF16)

        idx_now = sb("idx_now", [P, 2 * KT], U32)
        emb_next = sb("emb_next", [P, KT, 2, EMB])
        emb3 = sb("emb3", [P, KT, 3, EMB])
        emb_t = sb("emb_t", [P, TOK])
        emb_c = sb("emb_c", [P, KT, 2, EMB])
        lhs = sb("lhs", [P, 2, TOK])
        rhs = sb("rhs", [P, 2, D])
        gate_w = sb("gate_w", [P, 2, GATES])
        gate_x = sb("gate_x", [P, TOK])
        cov = sb("cov", [P, 2, EMB])
        quad = sb("quad", [P, KT, 2, EMB])
        scaled = sb("scaled", [P, 2, KT, 2, EMB])
        var1 = sb("var1", [P, KT, 2])
        stat = sb("stat", [P, 8, KT, 2])
        mix = sb("mix", [P, 2, 4, TOK])
        gate_y = sb("gate_y", [P, 2, TOK])
        bn6 = sb("bn6", [P, 2 * KT, 6])
        mean_var = sb("mean_var", [P, 2 * KT, 2])
        table_seen = sb("table_seen", [P, 1])
        stats_seen = sb("stats_seen", [P, 4])
        stat3 = sb("stat3", [P, 2, 4, KT])
        res = sb("res", [P, 2, KT, D])
        xt = sb("xt", [P, 2, 2, KD, TOK], BF16)

        x_f32 = (gate_y[:, 0, :], gate_y[:, 1, :])
        PS = len(x_f32)

        w_hi = sb("w_hi", [P, UNITS + 1, UW], BF16)
        w_lo = sb("w_lo", [P, UNITS + 1, UW], BF16)
        w_next = sb("w_next", [P, UW])
        w_raw = sb("w_raw", [P, UW])
        w_norm = sb("w_norm", [P, UW])
        q_mag = sb("q_mag", [P, RING, UW])
        q_int = sb("q_int", [P, RING, UW], BF16)
        q_dif = sb("q_dif", [P, RING, UW])
        err = sb("err", [P, NS, NB])
        pick = sb("pick", [P, 2, NS, NB])
        qs = sb("qs", [P, 8, NB])
        w_scaled = sb("w_scaled", [P, UW])
        w_clip = sb("w_clip", [P, UW])
        w_q = sb("w_q", [P, UW])

        g_hi = sb("g_hi", [P, ZR, TOK], BF16)
        g_lo = sb("g_lo", [P, ZR, TOK], BF16)
        mlp_f32 = mix[:].rearrange("p e j t -> p (e j) t")
        relu_z = mlp_f32[:, 0:ZR, :]
        act_g = mlp_f32[:, ZR:2 * ZR, :]
        bias_f32 = mlp_f32[:, 0:4, :]
        bias_bf = xt[:, 0, 0, 0:3, :]

        bank = [ctx.enter_context(nc.psum_tensor(f"bank{i}", [P, 512], F32)) for i in range(8)]
        Q_BANK = R1_BANK = 7
        QUAD_BANK = R12_BANK = 0
        PROJ_BANK, SKIP_BANK = 1, 3
        COV_BANK = SWAP_BANK = 2
        GATE_BANK = ((4, 5, 6), (0, 1, 3))
        TILE_BANK = (4, 5, 6)
        TR = len(TILE_BANK)
        XT_BANK = (6, 4, 5, 0, 6, 4, 5, 6)

        consts_in = sem("consts_in")
        idx_in = sem("idx_in")
        pool_const = sem("pool_const")
        zero_gate = sem("zero_gate")
        bias_part = sem("bias_part")
        bias_done = sem("bias_done")
        cin_ps = sem("cin_ps")
        wg_ready = sem("wg_ready")
        wmean_ps = sem("wmean_ps")
        wc_ready = sem("wc_ready")
        cin_ready = sem("cin_ready")
        emb_in = sem("emb_in")
        idx_ready = sem("idx_ready")
        emb3_ready = sem("emb3_ready")
        mean_ps = sem("mean_ps")
        et_ps = sem("et_ps")
        et_sb = sem("et_sb")
        emb_c_ready = sem("emb_c_ready")
        cov_ps = sem("cov_ps")
        cov_sb = sem("cov_sb")
        quad_ps = sem("quad_ps")
        proj_ps = sem("proj_ps")
        swap_ps = sem("swap_ps")
        front_ready = sem("front_ready")
        var1_ready = sem("var1_ready")
        r12_ready = sem("r12_ready")
        scaled_ready = sem("scaled_ready")
        scaled_ps = sem("scaled_ps")
        gates_ps = sem("gates_ps")
        alpha_ready = sem("alpha_ready")
        tanh_ready = sem("tanh_ready")
        y_ready = sem("y_ready")
        h2_ps = sem("h2_ps")
        h2_sb = sem("h2_sb")
        mv_ready = sem("mv_ready")
        r3_ready = sem("r3_ready")
        x2_ready = sem("x2_ready")
        xt_ps = sem("xt_ps")
        xf_ready = sem("xf_ready")
        xt_hi = sem("xt_hi")
        xt_lo = sem("xt_lo")
        stored = [sem("stored0"), sem("stored1")]
        stage_free = [sem("stage_free0"), sem("stage_free1")]
        w_in_sem = sem("w_landed")
        q_norm = sem("q_norm")
        q_rounded = sem("q_rounded")
        q_int_ready = sem("q_int_ready")
        q_dif_ready = sem("q_dif_ready")
        q_sq_ready = sem("q_sq_ready")
        err_ready = sem("err_ready")
        w_kept = sem("w_kept")
        scale_ready = sem("scale_ready")
        w_scaled_ready = sem("w_scaled_ready")
        clip_ready = sem("clip_ready")
        w_q_ready = sem("w_q_ready")
        w_t_ps = sem("w_t_ps")
        w_hi_ready = sem("w_hi_ready")
        w_lo_ready = sem("w_lo_ready")
        dve_step = sem("dve_step")
        pool_step = sem("pool_step")
        pool_pro = sem("pool_pro")
        x_in = [sem("x_in0"), sem("x_in1")]
        acc_in = [sem("acc_in0"), sem("acc_in1")]
        r3_part = sem("r3_part")
        quad_done = sem("quad_done")
        drive_done = sem("drive_done")
        scan_done = sem("scan_done")
        bn_done = sem("bn_done")
        acc_out = [sem("acc_out0"), sem("acc_out1")]
        z_ps = sem("z_ps")
        relu_ready = sem("relu_ready")
        g_ready = sem("g_ready")
        g_hi_ready = sem("g_hi_ready")
        g_lo_ready = sem("g_lo_ready")
        o_ps = sem("o_ps")
        o_added = sem("o_added")

        def blocks(ap):
            return ap.rearrange("p (b e) -> p b e", e=QB)

        def per_block(ap):
            return ap.unsqueeze(2).to_broadcast([P, NB, QB])

        def w_load(eng, u):
            eng.dma_start(w_next[:, 0:HALF], w_fc[bass.ds(u, 1), :, :].rearrange("a p n -> p (a n)")).then_inc(w_in_sem, 16)
            eng.dma_start(w_next[:, HALF:UW], w_proj[bass.ds(u, 1), :, :].rearrange("a p n -> p (a n)")).then_inc(w_in_sem, 16)

        def act_w_load(act, u):
            act.wait_ge(q_norm, u + 1)
            act.wait_ge(w_kept, u + 1)
            w_load(act, u + 1)

        def act_round(act, u, s):
            if s == 0:
                act.wait_ge(q_norm, u + 1)
            if s >= RING:
                act.wait_ge(q_int_ready, u * (NS - 1) + s - RING + 1)
            act.activation(q_mag[:, s % RING, :], w_norm[:], ACT.Identity, bias=magic[:, 0:1],
                           scale=1.0 / SHRINKS[s]).then_inc(q_rounded, 1)

        def act_square(act, u, s):
            act.wait_ge(q_dif_ready, u * NS + s + 1)
            act.activation(q_dif[:, s % RING, :], q_dif[:, s % RING, :], ACT.Square).then_inc(q_sq_ready, 1)

        def act_shrink(act, u, s):
            if s == 0:
                act_round(act, u, 0)
            if 2 <= s < NS + 2:
                act_square(act, u, s - 2)
            if s + 1 < NS:
                act_round(act, u, s + 1)

        def slot(t, u):
            return t[:, bass.ds(u + 1, 1), :].rearrange("p a n -> p (a n)")

        def act_weights(act, m):
            act.wait_ge(w_t_ps, m + 1)
            act.activation(slot(w_hi, m - 1), bank[Q_BANK][:], ACT.Copy).then_inc(w_hi_ready, 1)

        def dve_link(dve, ins, base, n):
            ins.then_inc(dve_step, 1)
            dve.wait_ge(dve_step, base + n)

        QSTEPS = 13

        def dve_norm(dve, u, n=1):
            base = u * QSTEPS
            dve.wait_ge(w_in_sem, u * 32 + 32)
            dve_link(dve, dve.tensor_scalar(w_norm[:].bitcast(U32), w_next[:].bitcast(U32), 0x7FFFFFFF, None, ALU.bitwise_and), base, n)
            dve_link(dve, dve.tensor_reduce(qs[:, 0, :], blocks(w_norm[:]), AX, ALU.max), base, n + 1)
            dve_link(dve, dve.tensor_scalar(qs[:, 1, :], qs[:, 0, :], 1e-8, 1.0 / QMAX, ALU.max, ALU.mult), base, n + 2)
            dve_link(dve, dve.reciprocal(qs[:, 2, :], qs[:, 1, :]), base, n + 3)
            dve.tensor_tensor(blocks(w_norm[:]), blocks(w_norm[:]), per_block(qs[:, 2, :]), ALU.mult).then_inc(q_norm, 1)

        def dve_shrink(dve, u, s):
            if s < NS - 1:
                dve.wait_ge(q_rounded, u * NS + s + 1)
                dve.tensor_scalar(q_int[:, s % RING, :], q_mag[:, s % RING, :], MAGIC + QMAX, MAGIC, ALU.min,
                                  ALU.subtract).then_inc(q_int_ready, 1)
            if 1 <= s < NS + 1:
                r = s - 1
                if r >= RING:
                    dve.wait_ge(err_ready, u * NS + r - RING + 1)
                if r < NS - 1:
                    dve.wait_ge(q_int_ready, u * (NS - 1) + r + 1)
                    dve.scalar_tensor_tensor(out=q_dif[:, r % RING, :], in0=q_int[:, r % RING, :], scalar=SHRINKS[r],
                                             in1=w_norm[:], op0=ALU.mult, op1=ALU.subtract).then_inc(q_dif_ready, 1)
                else:
                    dve.wait_ge(q_rounded, u * NS + r + 1)
                    dve.scalar_tensor_tensor(out=q_dif[:, r % RING, :], in0=q_mag[:, r % RING, :], scalar=MAGIC,
                                             in1=w_norm[:], op0=ALU.subtract, op1=ALU.subtract).then_inc(q_dif_ready, 1)
            if 3 <= s < NS + 3:
                r = s - 3
                dve.wait_ge(q_sq_ready, u * NS + r + 1)
                dve.tensor_reduce(err[:, r, :], blocks(q_dif[:, r % RING, :]), AX, ALU.add).then_inc(err_ready, 1)

        def dve_select(dve, u):
            base = u * QSTEPS
            by_block = err[:].rearrange("p s b -> p b s")
            dve.wait_ge(err_ready, u * NS + NS)
            dve_link(dve, dve.tensor_reduce(qs[:, 3, :], by_block, AX, ALU.min), base, 6)
            least = qs[:, 3, :].unsqueeze(1).to_broadcast([P, NS, NB])
            rank = shrink_rank[:].unsqueeze(2).to_broadcast([P, NS, NB])
            value = shrink_val[:].unsqueeze(2).to_broadcast([P, NS, NB])
            dve_link(dve, dve.tensor_tensor(pick[:, 0, :, :], err[:], least, ALU.is_equal), base, 7)
            dve_link(dve, dve.tensor_tensor(pick[:, 1, :, :], pick[:, 0, :, :], rank, ALU.mult), base, 8)
            dve_link(dve, dve.tensor_reduce(qs[:, 4, :], pick[:, 1, :, :].rearrange("p s b -> p b s"), AX, ALU.max), base, 9)
            first = qs[:, 4, :].unsqueeze(1).to_broadcast([P, NS, NB])
            dve_link(dve, dve.tensor_tensor(pick[:, 0, :, :], pick[:, 1, :, :], first, ALU.is_equal), base, 10)
            dve_link(dve, dve.tensor_tensor(pick[:, 1, :, :], pick[:, 0, :, :], value, ALU.mult), base, 11)
            dve_link(dve, dve.tensor_reduce(qs[:, 5, :], pick[:, 1, :, :].rearrange("p s b -> p b s"), AX, ALU.max), base, 12)
            dve_link(dve, dve.tensor_tensor(qs[:, 6, :], qs[:, 5, :], qs[:, 1, :], ALU.mult), base, 13)
            dve.reciprocal(qs[:, 7, :], qs[:, 6, :]).then_inc(scale_ready, 1)

        def dve_clip(dve, m, n=5):
            dve.wait_ge(w_scaled_ready, m + 1)
            dve_link(dve, dve.tensor_scalar(w_clip[:], w_scaled[:], MAGIC, MAGIC + QMAX, ALU.add, ALU.min), m * QSTEPS, n)
            dve.tensor_scalar(w_scaled[:], w_clip[:], MAGIC - QMAX, MAGIC, ALU.max, ALU.subtract).then_inc(clip_ready, 1)

        def dve_weights(dve, m):
            dve.wait_ge(w_hi_ready, m + 1)
            dve.tensor_tensor(slot(w_lo, m - 1), bank[Q_BANK][:], slot(w_hi, m - 1), ALU.subtract).then_inc(w_lo_ready, 1)

        def pool_link(pool, ins, base, n):
            ins.then_inc(pool_step, 1)
            pool.wait_ge(pool_step, base + n)

        def pool_dequant(pool, m, base, n):
            pool.wait_ge(clip_ready, m + 1)
            pool_link(pool, pool.tensor_tensor(blocks(w_clip[:]), blocks(w_scaled[:]), per_block(qs[:, 6, :]), ALU.mult), base, n)
            pool_link(pool, pool.tensor_tensor(w_clip[:], w_clip[:], w_raw[:], ALU.subtract), base, n + 1)
            pool.tensor_tensor(w_q[:], w_raw[:], w_clip[:], ALU.add).then_inc(w_q_ready, 1)

        def pool_keep(pool, u):
            pool.wait_ge(w_q_ready, u + 1)
            pool.wait_ge(w_in_sem, u * 32 + 32)
            pool.tensor_tensor(w_raw[:], w_next[:], one[:].to_broadcast([P, UW]), ALU.mult).then_inc(w_kept, 1)

        def pool_scale(pool, u):
            pool.wait_ge(scale_ready, u + 1)
            pool.tensor_tensor(blocks(w_scaled[:]), blocks(w_raw[:]), per_block(qs[:, 7, :]), ALU.mult).then_inc(w_scaled_ready, 1)

        def pe_weights(pe, m):
            pe.wait_ge(w_q_ready, m + 1)
            for k in range(UT):
                last = pe.transpose(bank[Q_BANK][:, k * P:(k + 1) * P], w_q[:, k * P:(k + 1) * P], ident[:])
            last.then_inc(w_t_ps, 1)

        block = ctx.enter_context(nc.Block())

        @block.sync
        def _(sp):
            sp.dma_start(idx[:], ids).then_inc(idx_in, 16)
            w_load(sp, 0)
            w_in_v = w_in.rearrange("(k p) n -> p k n", p=P)
            w_skip_v = w_skip.rearrange("(k p) n -> p k n", p=P)
            sp.dma_start(wc[:, :, 0:GATES], w_in_v).then_inc(consts_in, 16)
            sp.dma_start(wc[:, :, GATES:GATES + D], w_skip_v).then_inc(consts_in, 16)
            sp.dma_start(gamma_sb[:], gamma).then_inc(consts_in, 16)
            sp.dma_start(beta_sb[:], beta).then_inc(consts_in, 16)
            sp.dma_start(b_in_sb[:], b_in).then_inc(consts_in, 16)
            sp.dma_start(w_out_sb[:], w_out).then_inc(consts_in, 16)
            sp.dma_start(bias_f32[:, 0, :], b_out.partition_broadcast(P)).then_inc(consts_in, 16)
            sp.dma_start(bias_f32[:, 1, :], b_skip.partition_broadcast(P)).then_inc(consts_in, 16)

            def store_x(i, e):
                sp.wait_ge(xt_hi, i * 2 * KD + (e + 1) * KD + KD)
                sp.wait_ge(xt_lo, i * 2 * KD + (e + 1) * KD + KD)
                sp.dma_start(xt_dram[bass.ds(i * 2 + e, 1), :, :].rearrange("a p n -> p (a n)"),
                             xt[:, e].rearrange("p a k t -> p (a k t)")).then_inc(stored[e], 16)

            with sp.Fori(0, PAIRS - 1) as i:
                for e in range(2):
                    store_x(i, e)
                    sp.dma_start(acc_dram[bass.ds(i * 2 + e, 1), :, :].rearrange("a p n -> p (a n)"),
                                 res[:, e].rearrange("p k d -> p (k d)")).then_inc(stored[e], 16)
                for e in range(2):
                    sp.wait_ge(stored[e], i * 32 + 32)
                    sp.nop().then_inc(stage_free[e], 1)
            for e in range(2):
                store_x(PAIRS - 1, e)
                sp.nop().then_inc(x_in[e], 16)
                sp.nop().then_inc(acc_in[e], 16)
            for e in range(2):
                sp.wait_ge(stored[e], (PAIRS - 1) * 32 + 16)

            def load_x(g, e):
                sp.dma_start(xt[:, e].rearrange("p a k t -> p (a k t)"),
                             xt_dram[bass.ds(g, 1), :, :].rearrange("a p n -> p (a n)")).then_inc(x_in[e], 16)

            def load_acc(g, e):
                sp.dma_start(res[:, e].rearrange("p k d -> p (k d)"),
                             acc_dram[bass.ds(g, 1), :, :].rearrange("a p n -> p (a n)")).then_inc(acc_in[e], 16)

            def after_group(n, g, g_next, e, to_out):
                if g_next is not None:
                    sp.wait_ge(z_ps, n * 2 * HC + (e + 1) * HC)
                    load_x(g_next, e)
                sp.wait_ge(o_added, n * 2 * KT + KT * (e + 1) + KT)
                if to_out:
                    sp.dma_start(out[bass.ds(g, 1), :, :].rearrange("a (k p) d -> p (a k) d", p=P),
                                 res[:, e]).then_inc(acc_out[e], 16)
                else:
                    sp.dma_start(acc_dram[bass.ds(g, 1), :, :].rearrange("a p n -> p (a n)"),
                                 res[:, e].rearrange("p k d -> p (k d)")).then_inc(acc_out[e], 16)
                sp.wait_ge(acc_out[e], n * 16 + 16)
                if g_next is not None:
                    load_acc(g_next, e)

            for ph in range(PHASES):
                last_phase = ph == PHASES - 1
                for e in range(2):
                    after_group(ph * PAIRS, SEQS - 2 + e, e, e, last_phase)
                with sp.Fori(1, PAIRS - 1) as i:
                    for e in range(2):
                        after_group(i + ph * PAIRS, i * 2 - 2 + e, i * 2 + e, e, last_phase)
                for e in range(2):
                    after_group(ph * PAIRS + PAIRS - 1, SEQS - 4 + e, None if last_phase else SEQS - 2 + e, e, last_phase)

        @block.gpsimd
        def _(pool):
            pool.memset(ident[:], 0.0).then_inc(pool_pro, 1)
            pool.wait_ge(pool_pro, 1)
            pool.affine_select(out=ident[:], in_=ident[:], compare_op=ALU.not_equal, fill=1.0, base=0,
                               pattern=[[-1, P]], channel_multiplier=1).then_inc(pool_const, 1)
            pool.memset(ones_bf[:], 1.0)
            pool.memset(ones_mean[:], 1.0 / TOK).then_inc(pool_const, 1)
            pool.memset(magic[:], MAGIC).then_inc(pool_const, 1)
            for s in range(NS):
                pool.memset(shrink_val[:, s:s + 1], SHRINKS[s])
                pool.memset(shrink_rank[:, s:s + 1], float(NS - s)).then_inc(pool_const, 1)
            for t in (w_raw, w_q):
                pool.memset(t[:], 0.0)
            pool.memset(w_scaled[:], 0.0).then_inc(w_scaled_ready, 1)
            pool.memset(eps[:], EPS)
            pool.memset(neg_one[:], -1.0)
            pool.memset(one[:], 1.0)
            pool.memset(neg_half[:], -0.5).then_inc(pool_pro, 1)
            pool.wait_ge(pool_pro, 2)

            def gather(p, e):
                if e == 0:
                    pool.tensor_copy(idx_now[:], idx[:, bass.ds(p * 2 * KT, 2 * KT)]).then_inc(idx_ready, 1)
                    pool.wait_ge(idx_ready, p + 1)
                    pool.tensor_tensor(idx_seen[:], neg_one[:, 0:1], neg_one[:, 0:1], ALU.mult)
                for k in range(KT):
                    pool.indirect_dma_start(emb_next[:, k, e, :], None, table,
                                            bass.IndirectOffsetOnAxis(ap=idx_now[:, e * KT + k:e * KT + k + 1], axis=0)
                                            ).then_inc(emb_in, 16)

            def take_embeddings(p):
                pool.wait_ge(emb_in, p * 2 * KT * 16 + 2 * KT * 16)
                pool.tensor_tensor(emb3[:, :, 0:2, :], emb_next[:], one[:].unsqueeze(2).unsqueeze(3).to_broadcast([P, KT, 2, EMB]),
                                   ALU.mult)
                pool.tensor_tensor(emb3[:, :, 2, :], emb_next[:, :, 0, :], one[:].unsqueeze(2).to_broadcast([P, KT, EMB]),
                                   ALU.mult).then_inc(emb3_ready, 1)

            POOL_STEPS = 2 + 6 + 2 * 2
            TAIL_STEPS = 2
            FRONT_STEPS = 6

            def rsqrt_pair(base):
                pool_link(pool, pool.tensor_tensor(stat[:, 0], var1[:], eps[:], ALU.add), base, 1)
                pool_link(pool, pool.tensor_tensor(stat[:, 1], stat[:, 0], neg_half[:], ALU.pow), base, 2)
                pool_link(pool, pool.tensor_tensor(stat[:, 2], var1[:], stat[:, 1], ALU.mult), base, 3)
                pool_link(pool, pool.tensor_tensor(stat[:, 3], stat[:, 2], stat[:, 1], ALU.mult), base, 4)
                pool_link(pool, pool.tensor_tensor(stat[:, 4], stat[:, 3], eps[:], ALU.add), base, 5)
                pool_link(pool, pool.tensor_tensor(stat[:, 5], stat[:, 4], neg_half[:], ALU.pow), base, 6)
                pool.tensor_tensor(stat[:, 6], stat[:, 5], stat[:, 1], ALU.mult).then_inc(r12_ready, 1)

            def scale_embeddings(p):
                for which, r in ((1, 1), (0, 6)):
                    if r == 6:
                        pool.wait_ge(r12_ready, p + 1)
                    pool.tensor_tensor(scaled[:, which], emb3[:, :, 0:2, :], stat[:, r].unsqueeze(3).to_broadcast([P, KT, 2, EMB]),
                                       ALU.mult).then_inc(scaled_ready, 1)

            def rsqrt_mlp(i, e, base):
                pool.wait_ge(mv_ready, i * 2 + e + 1)
                mv = mean_var[:, e * KT:(e + 1) * KT, :]
                pool_link(pool, pool.tensor_tensor(stat3[:, e, 0, :], mv[:, :, 1], eps[:, :, 0], ALU.add), base, 1)
                pool_link(pool, pool.tensor_tensor(stat3[:, e, 1, :], stat3[:, e, 0, :], neg_half[:, :, 0], ALU.pow), base, 2)
                pool.tensor_tensor(stat3[:, e, 2, :], mv[:, :, 0], neg_one[:], ALU.mult).then_inc(r3_part, 1)
                pool.wait_ge(r3_part, i * 2 + e + 1)
                pool.tensor_tensor(stat3[:, e, 3, :], stat3[:, e, 2, :], stat3[:, e, 1, :], ALU.mult).then_inc(r3_ready, 1)

            def normalise(i, e):
                pool.wait_ge(r3_ready, 2 * i + e + 1)
                pool.wait_ge(h2_sb, 2 * KT * i + (e + 1) * KT)
                pool.tensor_tensor(stats_seen[:, 2 + e:3 + e], neg_one[:, 0:1], neg_one[:, 0:1], ALU.mult)
                for k in range(KT):
                    last = pool.tensor_scalar(mix[:, e, k, :], res[:, e, k, :], stat3[:, e, 1, k:k + 1], stat3[:, e, 3, k:k + 1],
                                              ALU.mult, ALU.add)
                last.then_inc(x2_ready, 1)

            pool.wait_ge(idx_in, 16)
            gather(0, 0)
            gather(0, 1)
            take_embeddings(0)
            pool.wait_ge(emb3_ready, 1)
            gather(1, 0)
            gather(1, 1)
            pool.wait_ge(var1_ready, 1)
            rsqrt_pair(0)
            scale_embeddings(0)
            pool.wait_ge(swap_ps, 1)
            pool.wait_ge(scaled_ready, 2)
            take_embeddings(1)

            def mixer_step(i, front, more):
                base = i * POOL_STEPS + FRONT_STEPS
                for e in range(2):
                    pool.wait_ge(scan_done, 2 * i + e + 1)
                    pool.wait_ge(tanh_ready, 2 * i + e + 1)
                    pool.tensor_tensor(gate_y[:, e, :], mix[:, e, 3, :], gate_y[:, e, :], ALU.mult).then_inc(y_ready, 1)
                pool_dequant(pool, i, base, 1)
                pool_keep(pool, i)
                if more:
                    pool.wait_ge(emb3_ready, i + 2)
                    gather(i + 2, 0)
                rsqrt_mlp(i, 0, base + 2)
                normalise(i, 0)
                if front:
                    pool.wait_ge(var1_ready, i + 2)
                    rsqrt_pair(base + 4)
                    scale_embeddings(i + 1)
                rsqrt_mlp(i, 1, base + (10 if front else 4))
                normalise(i, 1)
                if more:
                    gather(i + 2, 1)
                for d in range(PS):
                    pool.wait_ge(xf_ready, PS * i + d + 1)
                    pool.tensor_tensor(xt[:, 1, 1, d, :], x_f32[d], xt[:, 1, 0, d, :], ALU.subtract).then_inc(xt_lo, 1)
                if more:
                    pool.wait_ge(swap_ps, i + 2)
                    pool.wait_ge(scaled_ready, 2 * i + 4)
                    take_embeddings(i + 2)
                pool_scale(pool, i)

            with pool.Fori(0, PAIRS - 2) as i:
                mixer_step(i, True, True)
            mixer_step(PAIRS - 2, True, False)
            mixer_step(PAIRS - 1, False, False)

            def low_part(n, k):
                pool.wait_ge(g_hi_ready, n * 2 * HC + k + 1)
                pool.tensor_tensor(g_lo[:, k % ZR, :], act_g[:, k % ZR, :], g_hi[:, k % ZR, :], ALU.subtract).then_inc(g_lo_ready, 1)

            def mlp_step(n, finish, quant):
                m = n + PAIRS
                if finish:
                    pool_dequant(pool, m, n * TAIL_STEPS + PAIRS * POOL_STEPS, 1)
                low_part(n, 0)
                if quant:
                    pool_keep(pool, m)
                for k in range(1, 2 * HC):
                    low_part(n, k)
                if quant:
                    pool_scale(pool, m)

            for ph in range(PHASES - 1):
                with pool.Fori(0, PAIRS) as i:
                    mlp_step(i + ph * PAIRS, True, True)
            mlp_step((PHASES - 1) * PAIRS, True, False)
            with pool.Fori(1, PAIRS) as i:
                mlp_step(i + (PHASES - 1) * PAIRS, False, False)

        @block.tensor
        def _(pe):
            pe.wait_ge(consts_in, 8 * 16)
            pe.wait_ge(pool_const, 3 + NS)
            for j in range(3):
                for k in range(KD):
                    last = pe.matmul(bank[0][:, j:j + 1], wc[:, k, j * S:(j + 1) * S], beta_sb[:, k:k + 1],
                                     start=(k == 0), stop=(k == KD - 1))
            last.then_inc(cin_ps, 1)

            def weight_means(b, first, last_column):
                for k in range(KD):
                    last = pe.matmul(bank[b][:, 0:last_column - first], ones_mean[:], wc[:, k, first:last_column],
                                     start=(k == 0), stop=(k == KD - 1))
                last.then_inc(wmean_ps, 1)

            def tile(k, at=0):
                return emb3[:, k, at:at + 2, :].rearrange("p a b -> p (a b)")

            def transpose_embeddings(p):
                pe.wait_ge(emb3_ready, p + 1)
                for k in range(KT):
                    last = pe.transpose(bank[Q_BANK][:, k * P:(k + 1) * P], tile(k), ident[:])
                last.then_inc(et_ps, 1)

            def mean(p):
                pe.wait_ge(emb3_ready, p + 1)
                for k in range(KT):
                    last = pe.matmul(bank[COV_BANK][:, 0:P], ones_mean[:], tile(k), start=(k == 0), stop=(k == KT - 1))
                last.then_inc(mean_ps, 1)

            def covariance(p):
                pe.wait_ge(emb_c_ready, p + 1)
                for k in range(KT):
                    both = emb_c[:, k].rearrange("p a b -> p (a b)")
                    last = pe.matmul(bank[COV_BANK][:, P:2 * P], both, both, start=(k == 0), stop=(k == KT - 1))
                last.then_inc(cov_ps, 1)

            def quadratic(p):
                pe.wait_ge(et_sb, p + 1)
                pe.wait_ge(cov_sb, p + 1)
                for k in range(KT):
                    last = pe.matmul(bank[QUAD_BANK][:, k * P:(k + 1) * P], emb_t[:, k * P:(k + 1) * P],
                                     cov[:].rearrange("p a b -> p (a b)"), start=True, stop=True)
                last.then_inc(quad_ps, 1)

            def project():
                for k in range(KT):
                    pe.matmul(bank[PROJ_BANK][:, 0:GATES], tile(k), wc[:, k, 0:GATES], start=(k == 0), stop=(k == KT - 1))
                    last = pe.matmul(bank[SKIP_BANK][:], tile(k), wc[:, k, GATES:GATES + D], start=(k == 0), stop=(k == KT - 1))
                last.then_inc(proj_ps, 1)
                for k in range(KT):
                    last = pe.transpose(bank[SWAP_BANK][:, k * P:(k + 1) * P], tile(k, 1), ident[:])
                last.then_inc(swap_ps, 1)

            def transpose_scaled(p):
                for b, which in ((R1_BANK, 1), (R12_BANK, 0)):
                    pe.wait_ge(scaled_ready, 2 * p + 2 - which)
                    for k in range(KT):
                        last = pe.transpose(bank[b][:, k * P:(k + 1) * P], scaled[:, which, k].rearrange("p a b -> p (a b)"), ident[:])
                    last.then_inc(scaled_ps, 1)

            transpose_embeddings(0)
            mean(0)
            pe.wait_ge(wg_ready, 1)
            weight_means(PROJ_BANK, 0, GATES)
            covariance(0)
            weight_means(SKIP_BANK, GATES, GATES + D)
            pe.wait_ge(cin_ready, 1)
            quadratic(0)
            pe.wait_ge(wc_ready, 1)
            project()
            pe.wait_ge(bias_done, 2)
            transpose_scaled(0)

            def residual(i, e):
                pe.wait_ge(y_ready, 2 * i + e + 1)
                for k in range(KT):
                    m = e * KT + k
                    o = bank[TILE_BANK[m % TR]][:]
                    if m >= TR:
                        pe.wait_ge(h2_sb, 2 * KT * i + m - TR + 1)
                    pe.matmul(o, ones_bf[:], bias3[:], start=True, stop=False)
                    pe.matmul(o, lhs[:, e, k * P:(k + 1) * P], rhs[:, e, :], start=False, stop=False)
                    pe.matmul(o, gate_y[:, e, k * P:(k + 1) * P], w_out_sb[:], start=False, stop=True).then_inc(h2_ps, 1)

            def transpose_x(i, e, front):
                pe.wait_ge(x2_ready, 2 * i + e + 1)
                for d in range(KD):
                    m = e * KD + d
                    if m < TR:
                        pe.wait_ge(h2_sb, 2 * KT * i + 2 * KT - TR + 1 + m)
                    elif m == KD - 1:
                        if front:
                            pe.wait_ge(var1_ready, i + 2)
                    else:
                        if m < 2 * KD - 1:
                            pe.wait_ge(xt_lo, 2 * KD * i + KD + m - KD + 1)
                        else:
                            pe.wait_ge(xf_ready, PS * i + 1)
                    for k in range(KT):
                        last = pe.transpose(bank[XT_BANK[m]][:, k * P:(k + 1) * P], mix[:, e, k, d * P:(d + 1) * P], ident[:])
                    last.then_inc(xt_ps, 1)

            def mixer_step(i, front):
                pe.wait_ge(front_ready, i + 1)
                pe.wait_ge(xt_lo, 2 * KD * i + KD)
                if front:
                    mean(i + 1)
                for e in range(2):
                    for j in range(3):
                        pe.matmul(bank[GATE_BANK[e][j]][:], gate_w[:, e, j * S:(j + 1) * S], gate_x[:],
                                  start=True, stop=True).then_inc(gates_ps, 1)
                if front:
                    transpose_embeddings(i + 1)
                    covariance(i + 1)
                residual(i, 0)
                if front:
                    pe.wait_ge(y_ready, 2 * i + 2)
                    quadratic(i + 1)
                pe_weights(pe, i)
                residual(i, 1)
                transpose_x(i, 0, front)
                if front:
                    project()
                    pe.wait_ge(w_lo_ready, i + 1)
                    pe.wait_ge(xt_lo, 2 * KD * i + 2 * KD)
                    transpose_scaled(i + 1)
                transpose_x(i, 1, front)

            with pe.Fori(0, PAIRS - 1) as i:
                mixer_step(i, True)
            mixer_step(PAIRS - 1, False)

            def up(n, unit0, e, c, last_unit):
                if c == 0:
                    pe.wait_ge(x_in[e], n * 16 + 16)
                z = bank[Z_BANK[(e * HC + c) % ZR]][:]
                for d in range(KD):
                    if last_unit and d == KD // 2:
                        pe.wait_ge(w_lo_ready, n + PAIRS + 1)
                    at, t = unit0 + 1 + 2 * c + d // 2, d % 2
                    hi, lo = w_hi[:, at, t * P:(t + 1) * P], w_lo[:, at, t * P:(t + 1) * P]
                    pe.matmul(z, hi, xt[:, e, 0, d, :], start=(d == 0), stop=False)
                    pe.matmul(z, hi, xt[:, e, 1, d, :], start=False, stop=False)
                    last = pe.matmul(z, lo, xt[:, e, 0, d, :], start=False, stop=(d == KD - 1))
                last.then_inc(z_ps, 1)

            def down(n, unit0, e, c):
                j, at = e * HC + c, unit0 + 1 + 2 * c
                w_h, w_l = w_hi[:, at:at + 2, HALF:UW], w_lo[:, at:at + 2, HALF:UW]
                pe.wait_ge(g_hi_ready, n * 2 * HC + j + 1)
                for k in range(KT):
                    o = bank[2 + k][:].rearrange("p (a b) -> p a b", b=HALF)
                    if c == 0:
                        pe.wait_ge(o_added, n * 2 * KT + e * KT + k + 1)
                    ghi = g_hi[:, j % ZR, k * P:(k + 1) * P]
                    pe.matmul(o, ghi, w_h, start=(c == 0), stop=False)
                    pe.matmul(o, ghi, w_l, start=False, stop=False)
                pe.wait_ge(g_lo_ready, n * 2 * HC + j + 1)
                for k in range(KT):
                    o = bank[2 + k][:].rearrange("p (a b) -> p a b", b=HALF)
                    last = pe.matmul(o, g_lo[:, j % ZR, k * P:(k + 1) * P], w_h, start=False, stop=(c == HC - 1))
                    if c == HC - 1:
                        last.then_inc(o_ps, 1)

            def mlp_step(ph, n, finish):
                def ups(*js):
                    for j in js:
                        up(n, ph * PAIRS, *divmod(j, HC), finish and j == HC - 1)

                def downs(*js):
                    for j in js:
                        down(n, ph * PAIRS, *divmod(j, HC))

                ups(0, 1, 2)
                downs(0)
                if finish:
                    pe_weights(pe, n + PAIRS)
                downs(1)
                ups(3, 4)
                for j in range(5, 2 * HC):
                    downs(j - ZR)
                    ups(j)
                downs(5, 6, 7)

            pe.wait_ge(xt_lo, 2 * KD * PAIRS + KD)
            for ph in range(PHASES):
                pe.wait_ge(w_lo_ready, (ph + 1) * PAIRS)
                if ph < PHASES - 1:
                    with pe.Fori(0, PAIRS) as i:
                        mlp_step(ph, i + ph * PAIRS, True)
                else:
                    mlp_step(ph, ph * PAIRS, True)
                    with pe.Fori(1, PAIRS) as i:
                        mlp_step(ph, i + ph * PAIRS, False)

        @block.scalar
        def _(act):
            for e in range(2):
                act.nop().then_inc(stage_free[e], 1)
            act.nop().then_inc(xt_hi, KD)
            act.wait_ge(pool_const, 3 + NS)
            act.wait_ge(cin_ready, 1)
            act.wait_ge(zero_gate, 1)

            def take_et(p):
                act.wait_ge(et_ps, p + 1)
                act.activation(emb_t[:], bank[Q_BANK][:], ACT.Copy).then_inc(et_sb, 1)

            def own(e):
                return slice(e * EMB, (e + 1) * EMB)

            def take_cov(p):
                act.wait_ge(cov_ps, p + 1)
                for e in range(2):
                    last = act.activation(cov[own(e), e, :], bank[COV_BANK][own(e), P + e * EMB:P + (e + 1) * EMB], ACT.Copy,
                                          scale=1.0 / (EMB * D))
                last.then_inc(cov_sb, 1)

            def take_projections(p):
                act.wait_ge(proj_ps, p + 1)
                for e in range(2):
                    act.activation(gate_w[own(e), e, :], bank[PROJ_BANK][own(e), 0:GATES], ACT.Copy, scale=0.125)
                    act.activation(rhs[own(e), e, :], bank[SKIP_BANK][own(e), :], ACT.Copy, scale=0.125)

            def take_swapped(p):
                act.wait_ge(swap_ps, p + 1)
                for e in range(2):
                    act.activation(lhs[own(1 - e), e, :], bank[SWAP_BANK][own(1 - e), :], ACT.Copy)
                    last = act.activation(rhs[own(1 - e), e, :], bank[SWAP_BANK][own(1 - e), :], ACT.Copy, scale=0.125)
                last.then_inc(front_ready, 1)

            def take_scaled(p):
                act.wait_ge(scaled_ps, 2 * p + 1)
                for e in range(2):
                    act.activation(lhs[own(e), e, :], bank[R1_BANK][own(e), :], ACT.Copy)
                act.wait_ge(scaled_ps, 2 * p + 2)
                act.activation(gate_x[:], bank[R12_BANK][:], ACT.Copy)

            def take_residual(i, m):
                e, k = divmod(m, KT)
                if k == 0:
                    act.wait_ge(stage_free[e], i + 1)
                act.wait_ge(h2_ps, 2 * KT * i + m + 1)
                act.activation(res[:, e, k, :], bank[TILE_BANK[m % TR]][:], ACT.Copy).then_inc(h2_sb, 1)

            def high_parts(i, e, slices):
                for d in slices:
                    m = e * KD + d
                    act.wait_ge(xt_ps, 2 * KD * i + m + 1)
                    act.activation(xt[:, e, 0, d, :], bank[XT_BANK[m]][:], ACT.Copy).then_inc(xt_hi, 1)
                    if e == 1 and d < PS:
                        act.activation(x_f32[d], bank[XT_BANK[m]][:], ACT.Copy).then_inc(xf_ready, 1)

            take_et(0)
            take_cov(0)
            take_projections(0)
            take_scaled(0)
            take_swapped(0)

            def mixer_step(i, front):
                act.activation(table_seen[:], magic[:], ACT.Sigmoid)
                act_shrink(act, i, 0)
                act_shrink(act, i, 1)
                for e in range(2):
                    b0, _, b2 = GATE_BANK[e]
                    act.wait_ge(gates_ps, 6 * i + 3 * e + 3)
                    act.activation(mix[:, e, 0, :], bank[b0][:], ACT.Sigmoid, bias=c_in[:, 0:1]).then_inc(alpha_ready, 1)
                    if e == 0:
                        act.wait_ge(xt_lo, 2 * KD * i + KD)
                    act.activation(gate_y[:, e, :], bank[b2][:], ACT.Tanh, bias=c_in[:, 2:3]).then_inc(tanh_ready, 1)
                    if front and e == 0:
                        take_et(i + 1)
                    act_shrink(act, i, 2 + e)
                if front:
                    take_cov(i + 1)
                act_shrink(act, i, 4)
                take_residual(i, 0)
                act_shrink(act, i, 5)
                take_residual(i, 1)
                act_shrink(act, i, 6)
                take_residual(i, 2)
                act_shrink(act, i, 7)
                take_residual(i, 3)
                act_weights(act, i)
                take_residual(i, 4)
                act_shrink(act, i, 8)
                take_residual(i, 5)
                act_w_load(act, i)
                act_shrink(act, i, 9)
                take_residual(i, 6)
                take_residual(i, 7)
                act_shrink(act, i, 10)
                high_parts(i, 0, range(KD))
                act_shrink(act, i, 11)
                act_shrink(act, i, 12)
                if front:
                    take_projections(i + 1)
                act_shrink(act, i, 13)
                if front:
                    take_scaled(i + 1)
                act_shrink(act, i, 14)
                high_parts(i, 1, (0, 1))
                act_shrink(act, i, 15)
                high_parts(i, 1, (2, 3))
                act_shrink(act, i, 16)
                if front:
                    take_swapped(i + 1)
                for s in range(17, SLOTS):
                    act_shrink(act, i, s)

            with act.Fori(0, PAIRS - 1) as i:
                mixer_step(i, True)
            mixer_step(PAIRS - 1, False)

            def mlp_step(n, finish, quant, load):
                m = n + PAIRS
                for k in range(2 * HC):
                    act.wait_ge(z_ps, n * 2 * HC + k + 1)
                    act.activation(relu_z[:, k % ZR, :], bank[Z_BANK[k % ZR]][:], ACT.Relu).then_inc(relu_ready, 1)
                    act.wait_ge(relu_ready, n * 2 * HC + k + 1)
                    act.activation(act_g[:, k % ZR, :], relu_z[:, k % ZR, :], ACT.Square).then_inc(g_ready, 1)
                    if quant:
                        for s in SHRINK_SLOTS[k]:
                            act_shrink(act, m, s)
                    if k == 1 and finish:
                        act_weights(act, m)
                    if k == 3 and load:
                        act_w_load(act, m)

            for ph in range(PHASES - 1):
                if ph < PHASES - 2:
                    with act.Fori(0, PAIRS) as i:
                        mlp_step(i + ph * PAIRS, True, True, True)
                else:
                    with act.Fori(0, PAIRS - 1) as i:
                        mlp_step(i + ph * PAIRS, True, True, True)
                    mlp_step(ph * PAIRS + PAIRS - 1, True, True, False)
            mlp_step((PHASES - 1) * PAIRS, True, False, False)
            with act.Fori(1, PAIRS) as i:
                mlp_step(i + (PHASES - 1) * PAIRS, False, False, False)

        @block.vector
        def _(dve):
            dve.memset(qs[:], 0.0)
            for e in range(2):
                dve.memset(gate_w[(1 - e) * EMB:(2 - e) * EMB, e, :], 0.0)
                dve.memset(cov[(1 - e) * EMB:(2 - e) * EMB, e, :], 0.0)
            dve.memset(bias3[:], 0.0).then_inc(zero_gate, 1)
            dve.wait_ge(zero_gate, 1)
            dve.wait_ge(consts_in, 8 * 16)
            dve.wait_ge(cin_ps, 1)
            dve.tensor_tensor(c_in[:], bank[0][:, 0:3], b_in_sb[:], ALU.add).then_inc(cin_ready, 1)
            for k in range(KD):
                last = dve.tensor_scalar(wc[:, k, 0:GATES], wc[:, k, 0:GATES], gamma_sb[:, k:k + 1], None, ALU.mult)
            last.then_inc(wg_ready, 1)
            def bias_link(ins, n):
                ins.then_inc(bias_part, 1)
                dve.wait_ge(bias_part, n)

            bias_link(dve.tensor_tensor(bias_f32[:, 2, :], bias_f32[:, 0, :], bias_f32[:, 1, :], ALU.add), 1)
            bias_link(dve.tensor_copy(bias_bf[:, 0, :], bias_f32[:, 2, :]), 2)
            bias_link(dve.tensor_tensor(bias_f32[:, 3, :], bias_f32[:, 2, :], bias_bf[:, 0, :], ALU.subtract), 3)
            bias_link(dve.tensor_copy(bias_bf[:, 1, :], bias_f32[:, 3, :]), 4)
            bias_link(dve.tensor_tensor(bias_bf[:, 2, :], bias_f32[:, 3, :], bias_bf[:, 1, :], ALU.subtract), 5)
            for part in range(3):
                row = 32 * part
                last = dve.tensor_copy(bias3[row:row + 1, :], bias_bf[row:row + 1, part, :])
            last.then_inc(bias_done, 2)
            dve.nop().then_inc(o_added, KT)
            dve.nop().then_inc(xt_lo, KD)

            def centre(p):
                dve.wait_ge(mean_ps, p + 1)
                mean = bank[COV_BANK][:, 0:P].rearrange("p (a b) -> p a b", b=EMB).unsqueeze(1).to_broadcast([P, KT, 2, EMB])
                dve.tensor_tensor(emb_c[:], emb3[:, :, 0:2, :], mean, ALU.subtract).then_inc(emb_c_ready, 1)

            def variance(p):
                dve.wait_ge(quad_ps, p + 1)
                dve.tensor_tensor(quad[:], bank[QUAD_BANK][:].rearrange("p (k a b) -> p k a b", a=2, b=EMB), emb3[:, :, 0:2, :],
                                  ALU.mult).then_inc(quad_done, 1)
                dve.wait_ge(quad_done, p + 1)
                dve.tensor_reduce(var1[:], quad[:], AX, ALU.add).then_inc(var1_ready, 1)

            def statistics(i, m):
                dve.wait_ge(h2_sb, 2 * KT * i + m + 1)
                dve.bn_stats(bn6[:, m, :], res[:, m // KT, m % KT, :]).then_inc(bn_done, 1)

            def aggregate(i, e):
                dve.wait_ge(bn_done, 2 * KT * i + (e + 1) * KT)
                dve.tensor_scalar(stats_seen[:, e:e + 1], magic[:], 1.0, None, ALU.mult)
                for k in range(KT):
                    last = dve.bn_aggr(mean_var[:, e * KT + k, :], bn6[:, e * KT + k, :])
                last.then_inc(mv_ready, 1)

            def low_parts(i, e, slices):
                for d in slices:
                    m = e * KD + d
                    dve.wait_ge(xt_hi, 2 * KD * i + m + 1 + KD)
                    dve.tensor_tensor(xt[:, e, 1, d, :], bank[XT_BANK[m]][:], xt[:, e, 0, d, :], ALU.subtract).then_inc(xt_lo, 1)

            centre(0)
            dve.wait_ge(wg_ready, 1)
            dve.wait_ge(wmean_ps, 1)
            for k in range(KD):
                dve.tensor_tensor(wc[:, k, 0:GATES], wc[:, k, 0:GATES], bank[PROJ_BANK][:, 0:GATES], ALU.subtract)
            dve.wait_ge(wmean_ps, 2)
            for k in range(KD):
                last = dve.tensor_tensor(wc[:, k, GATES:GATES + D], wc[:, k, GATES:GATES + D], bank[SKIP_BANK][:], ALU.subtract)
            last.then_inc(wc_ready, 1)
            variance(0)
            dve.wait_ge(pool_const, 3 + NS)

            def mixer_step(i, front):
                dve_norm(dve, i)
                dve_clip(dve, i)
                dve_shrink(dve, i, 0)
                dve_shrink(dve, i, 1)
                if front:
                    centre(i + 1)
                for e in range(2):
                    b1 = GATE_BANK[e][1]
                    alpha, keep, drive, state = (mix[:, e, j, :] for j in range(4))
                    dve.wait_ge(alpha_ready, 2 * i + e + 1)
                    dve.tensor_scalar(keep, alpha, -1.0, 1.0, ALU.mult, ALU.add)
                    dve.scalar_tensor_tensor(out=drive, in0=bank[b1][:], scalar=c_in[:, 1:2], in1=alpha, op0=ALU.add,
                                             op1=ALU.mult).then_inc(drive_done, 1)
                    dve.wait_ge(drive_done, 2 * i + e + 1)
                    dve.tensor_tensor_scan(state, keep, drive, 0.0, ALU.mult, ALU.add).then_inc(scan_done, 1)
                    dve_shrink(dve, i, 2 + e)
                dve_shrink(dve, i, 4)
                for m in range(KT):
                    statistics(i, m)
                    if m < KT - 1:
                        dve_shrink(dve, i, 5 + m)
                aggregate(i, 0)
                if front:
                    variance(i + 1)
                dve_weights(dve, i)
                for m in range(KT, 2 * KT):
                    statistics(i, m)
                    if m < 2 * KT - 1:
                        dve_shrink(dve, i, 4 + m)
                aggregate(i, 1)
                low_parts(i, 0, range(KD))
                for s in range(11, 16):
                    dve_shrink(dve, i, s)
                low_parts(i, 1, range(PS, KD))
                for s in range(16, SLOTS):
                    dve_shrink(dve, i, s)
                dve_select(dve, i)

            with dve.Fori(0, PAIRS - 1) as i:
                mixer_step(i, True)
            mixer_step(PAIRS - 1, False)

            def add_group(n, e):
                dve.wait_ge(acc_in[e], n * 16 + 16)
                for k in range(KT):
                    dve.wait_ge(o_ps, n * 2 * KT + e * KT + k + 1)
                    dve.tensor_tensor(res[:, e, k, :], bank[2 + k][:], res[:, e, k, :], ALU.add).then_inc(o_added, 1)

            def mlp_step(n, finish, quant):
                m = n + PAIRS
                if finish:
                    dve_clip(dve, m, 1)
                if quant:
                    dve_norm(dve, m, 2)
                for k in range(2 * HC):
                    if k == HC + 1:
                        add_group(n, 0)
                    dve.wait_ge(g_ready, n * 2 * HC + k + 1)
                    dve.tensor_scalar(g_hi[:, k % ZR, :], act_g[:, k % ZR, :], 1.0, None, ALU.mult).then_inc(g_hi_ready, 1)
                    if quant:
                        for s in SHRINK_SLOTS[k]:
                            dve_shrink(dve, m, s)
                    if k == 1 and finish:
                        dve_weights(dve, m)
                if quant:
                    dve_select(dve, m)
                add_group(n, 1)

            for ph in range(PHASES - 1):
                with dve.Fori(0, PAIRS) as i:
                    mlp_step(i + ph * PAIRS, True, True)
            mlp_step((PHASES - 1) * PAIRS, True, False)
            with dve.Fori(1, PAIRS) as i:
                mlp_step(i + (PHASES - 1) * PAIRS, False, False)


def kernel(x, L0_tok_weight, L0_attn_gamma, L0_attn_beta, L0_attn_W_in, L0_attn_b_in, L0_attn_W_out, L0_attn_b_out,
           L0_attn_W_skip, L0_attn_b_skip, L0_ffn_w_fc, L0_ffn_w_proj):
    import concourse.bacc as bacc
    from concourse.bass_utils import run_bass_kernel_spmd

    arr = np.asarray
    halves = D // HALF
    arrays = {
        "ids": arr(x).reshape(SEQS * KT, P).T,
        "table": arr(L0_tok_weight),
        "gamma": arr(L0_attn_gamma).reshape(KD, P).T,
        "beta": arr(L0_attn_beta).reshape(KD, P).T,
        "w_in": arr(L0_attn_W_in),
        "b_in": arr(L0_attn_b_in).reshape(3, S).T,
        "w_out": arr(L0_attn_W_out),
        "b_out": arr(L0_attn_b_out),
        "w_skip": arr(L0_attn_W_skip),
        "b_skip": arr(L0_attn_b_skip),
        "w_fc": arr(L0_ffn_w_fc).reshape(PHASES, HC, P, halves, HALF).transpose(0, 1, 3, 2, 4).reshape(UNITS, P, HALF),
        "w_proj": arr(L0_ffn_w_proj).reshape(halves, KD // halves, P, PHASES, HC, P).transpose(3, 4, 0, 2, 1, 5)
        .reshape(UNITS, P, HALF),
    }
    arrays = {k: np.ascontiguousarray(v) for k, v in arrays.items()}
    nc = bacc.Bacc("TRN2", target_bir_lowering=False, num_devices=1)
    args = [nc.dram_tensor(k, v.shape, mybir.dt.uint32 if v.dtype.kind in "iu" else mybir.dt.from_np(v.dtype),
                           kind="ExternalInput").ap() for k, v in arrays.items()]
    out = nc.dram_tensor("out", (SEQS, TOK, D), F32, kind="ExternalOutput").ap()
    build(nc, *args, out)
    arrays["ids"] = arrays["ids"].view(np.uint32)
    got = run_bass_kernel_spmd(nc, [arrays], core_ids=[0])
    return got.results[0]["out"]
```
